# Optimizing a Trainium2 kernel written in Bass

```python
import numpy as np
import jax
import jax.numpy as jnp

def _softmax(x, axis=-1):
    return jax.nn.softmax(x, axis=axis)

def _gelu(x):
    return jax.nn.gelu(x, approximate=True)

def _silu(x):
    return jax.nn.silu(x)

def _sigmoid(x):
    return jax.nn.sigmoid(x)

def _layernorm(x, axis=-1, eps=1e-05):
    m = jnp.mean(x, axis=axis, keepdims=True)
    v = jnp.var(x, axis=axis, keepdims=True)
    return (x - m) / jnp.sqrt(v + eps)

def _scatter_add(tgt, idx, src, axis=0):
    return tgt.at[idx].add(src)

def _segment_sum(src, seg, n):
    return jax.ops.segment_sum(src, seg, n)
kernel_name = 'mk_gnn_ffn_d1_gnn_r8_ab80e1'

def setup_inputs(seed: int=0):
    np.random.seed(seed)
    _w = jnp.asarray

    def _rec_inputs():
        import jax
        import jax.numpy as jnp
        _gk = jax.random.key(seed)
        x = -0.0002117 + 1 * jax.random.normal(jax.random.fold_in(_gk, 1), (12500, 256), jnp.float32)
        _s = jax.random.randint(jax.random.fold_in(_gk, 2), (100000,), 0, 12500, jnp.int32)
        _d = jax.random.randint(jax.random.fold_in(_gk, 3), (100000,), 0, 12500, jnp.int32)
        _loop = jnp.arange(12500, dtype=jnp.int32)
        src = jnp.concatenate([_s, _d, _loop])
        dst = jnp.concatenate([_d, _s, _loop])
        _o = jnp.argsort(dst, stable=True)
        src = src[_o]
        dst = dst[_o]
        edge_weight = jax.random.uniform(jax.random.fold_in(_gk, 12), (212500,), jnp.float32, 0.0, 1)
        return (x, src, dst, edge_weight)
    x, src, dst, edge_weight = _rec_inputs()

    def _L0_gnn_setup():
        import jax, jax.numpy as jnp
        import numpy as np
        N_NODES = 12500
        N_EDGES = 400000
        D_IN = 256
        D_OUT = 256
        key = jax.random.key(seed)
        k1, k2, k3, k4, k5, k6 = jax.random.split(key, 6)
        X = jax.random.normal(k1, (N_NODES, D_IN), dtype=jnp.float32)
        edge_src = jax.random.randint(k2, (N_EDGES,), 0, N_NODES, dtype=jnp.int32)
        edge_dst = jax.random.randint(k3, (N_EDGES,), 0, N_NODES, dtype=jnp.int32)
        edge_val = jax.random.uniform(k4, (N_EDGES,), dtype=jnp.float32)
        stdv = 1.0 / np.sqrt(D_OUT)
        W = jax.random.uniform(k5, (D_IN, D_OUT), minval=-stdv, maxval=stdv, dtype=jnp.float32)
        b = jax.random.uniform(k6, (D_OUT,), minval=-stdv, maxval=stdv, dtype=jnp.float32)
        return {'X': X, 'edge_src': edge_src, 'edge_dst': edge_dst, 'edge_val': edge_val, 'W': W, 'b': b}
    _L0_gnn_all = _L0_gnn_setup()
    _L0_gnn_in = {k: v for k, v in _L0_gnn_all.items() if k in ('W', 'b')}
    del _L0_gnn_all

    def _L0_ffn_setup():
        import jax, jax.numpy as jnp
        import numpy as np
        BN_EPS = 0.001

        def _bn(h, g, b, m, v):
            return g * (h - m) * jax.lax.rsqrt(v + BN_EPS) + b
        key = jax.random.key(seed)
        ks = jax.random.split(key, 8)
        B, F, Df = (256, 64, 256)
        E, H, D = (8, 256, 256)
        s1 = 1.0 / np.sqrt(Df)
        s2 = 1.0 / np.sqrt(H)
        return {'x': jax.random.normal(ks[0], (B, F, Df), jnp.float32), 'Wr': jax.random.normal(ks[1], (Df, E), jnp.float32) * s1, 'br': jnp.zeros((E,), jnp.float32), 'W1': jax.random.normal(ks[2], (E, Df, H), jnp.float32) * s1, 'b1': jnp.zeros((E, H), jnp.float32), 'g1': jnp.ones((E, H), jnp.float32), 'be1': jnp.zeros((E, H), jnp.float32), 'm1': jnp.zeros((E, H), jnp.float32), 'v1': jnp.ones((E, H), jnp.float32), 'W2': jax.random.normal(ks[3], (E, H, H), jnp.float32) * s2, 'b2': jnp.zeros((E, H), jnp.float32), 'g2': jnp.ones((E, H), jnp.float32), 'be2': jnp.zeros((E, H), jnp.float32), 'm2': jnp.zeros((E, H), jnp.float32), 'v2': jnp.ones((E, H), jnp.float32), 'Wo': jax.random.normal(ks[4], (E, H, D), jnp.float32) * s2, 'bo': jnp.zeros((E, D), jnp.float32)}
    _L0_ffn_all = _L0_ffn_setup()
    _L0_ffn_in = {k: v for k, v in _L0_ffn_all.items() if k in ('Wr', 'br', 'W1', 'b1', 'g1', 'be1', 'm1', 'v1', 'W2', 'b2', 'g2', 'be2', 'm2', 'v2', 'Wo', 'bo')}
    del _L0_ffn_all
    return {'x': x, 'src': src, 'dst': dst, 'edge_weight': edge_weight, 'L0_gnn_W': _L0_gnn_in['W'], 'L0_gnn_b': _L0_gnn_in['b'], 'L0_ffn_Wr': _L0_ffn_in['Wr'], 'L0_ffn_br': _L0_ffn_in['br'], 'L0_ffn_W1': _L0_ffn_in['W1'], 'L0_ffn_b1': _L0_ffn_in['b1'], 'L0_ffn_g1': _L0_ffn_in['g1'], 'L0_ffn_be1': _L0_ffn_in['be1'], 'L0_ffn_m1': _L0_ffn_in['m1'], 'L0_ffn_v1': _L0_ffn_in['v1'], 'L0_ffn_W2': _L0_ffn_in['W2'], 'L0_ffn_b2': _L0_ffn_in['b2'], 'L0_ffn_g2': _L0_ffn_in['g2'], 'L0_ffn_be2': _L0_ffn_in['be2'], 'L0_ffn_m2': _L0_ffn_in['m2'], 'L0_ffn_v2': _L0_ffn_in['v2'], 'L0_ffn_Wo': _L0_ffn_in['Wo'], 'L0_ffn_bo': _L0_ffn_in['bo']}

def reference(x, src, dst, edge_weight, L0_gnn_W, L0_gnn_b, L0_ffn_Wr, L0_ffn_br, L0_ffn_W1, L0_ffn_b1, L0_ffn_g1, L0_ffn_be1, L0_ffn_m1, L0_ffn_v1, L0_ffn_W2, L0_ffn_b2, L0_ffn_g2, L0_ffn_be2, L0_ffn_m2, L0_ffn_v2, L0_ffn_Wo, L0_ffn_bo):
    import jax
    import jax.numpy as jnp

    def _L0_gnn_ref(X, edge_src, edge_dst, edge_val, W, b):
        import jax, jax.numpy as jnp
        import numpy as np
        N_NODES = 12500
        N_EDGES = 400000
        D_IN = 256
        D_OUT = 256
        support = X @ W
        msgs = support[edge_src] * edge_val[:, None]
        out = jax.ops.segment_sum(msgs, edge_dst, num_segments=N_NODES)
        return out + b

    def _L0_ffn_ref(x, Wr, br, W1, b1, g1, be1, m1, v1, W2, b2, g2, be2, m2, v2, Wo, bo):
        import jax, jax.numpy as jnp
        import numpy as np
        BN_EPS = 0.001

        def _bn(h, g, b, m, v):
            return g * (h - m) * jax.lax.rsqrt(v + BN_EPS) + b
        feat = jnp.mean(x, axis=0)
        w = jax.nn.softmax(feat @ Wr + br, axis=-1)
        h = jnp.einsum('bfd,edh->bfeh', x, W1) + b1
        h = jax.nn.relu(_bn(h, g1, be1, m1, v1))
        h = jnp.einsum('bfeh,ehk->bfek', h, W2) + b2
        h = jax.nn.relu(_bn(h, g2, be2, m2, v2))
        y = jnp.einsum('bfeh,ehd->bfed', h, Wo) + bo
        return jnp.einsum('bfed,fe->bfd', y, w)
    x = x + _L0_gnn_ref(_layernorm(x, axis=-1), src, dst, edge_weight, L0_gnn_W, L0_gnn_b)
    x = x + _L0_ffn_ref(_layernorm(x, axis=-1)[None], L0_ffn_Wr, L0_ffn_br, L0_ffn_W1, L0_ffn_b1, L0_ffn_g1, L0_ffn_be1, L0_ffn_m1, L0_ffn_v1, L0_ffn_W2, L0_ffn_b2, L0_ffn_g2, L0_ffn_be2, L0_ffn_m2, L0_ffn_v2, L0_ffn_Wo, L0_ffn_bo)[0]
    return x

_drawn_inputs = setup_inputs


def setup_inputs(seed=0):
    import zlib

    import numpy as np

    out = dict(_drawn_inputs(seed))
    spreads = {'L0_ffn_br': (0.0, 0.398),
     'L0_ffn_b1': (0.0, 0.533),
     'L0_ffn_g1': (1.0, 0.2),
     'L0_ffn_be1': (0.0, 0.541),
     'L0_ffn_m1': (0.0, 0.527),
     'L0_ffn_v1': (1.0, 0.6),
     'L0_ffn_b2': (0.0, 0.379),
     'L0_ffn_g2': (1.0, 0.2),
     'L0_ffn_be2': (0.0, 0.396),
     'L0_ffn_m2': (0.0, 0.392),
     'L0_ffn_v2': (1.0, 0.6),
     'L0_ffn_bo': (0.0, 0.284)}
    factors = {'L0_gnn_b': 2.677}
    for name, (base, spread) in spreads.items():
        noise = np.random.default_rng([zlib.crc32(name.encode()), seed]).standard_normal(out[name].shape)
        drawn = base * np.exp(spread * noise) if base else spread * noise
        out[name] = jnp.asarray(drawn.astype(out[name].dtype))
    for name, factor in factors.items():
        out[name] = (out[name] * factor).astype(out[name].dtype)
    return out
```

```python
from contextlib import ExitStack

import concourse.bass as bass
from concourse import mybir

F32 = mybir.dt.float32
F32R = mybir.dt.float32r
I32 = mybir.dt.int32
I16 = mybir.dt.int16
ALU = mybir.AluOpType
ACT = mybir.ActivationFunctionType
AX_X = mybir.AxisListType.X

P = 128
D = 256
KT = D // P
E = 8
N = 12500
NE = 212500
NT = 125
TILES = N // NT
GT = 4
GN = GT * NT
G = TILES // GT
C = 18
WIN = C * P
PC = 3
PT = C // PC
PG = PT * GT
PS = PG // E
GR = 8
SR = 4
AHEAD = 2
LEAD = PG + PG // 2
ROWS = 125
COLS = NE // ROWS
XN = 5
XC = N // NT // XN
XB = 8
LN_EPS = 1e-5
BN_EPS = 1e-3
NPAR = 5


def gnn_experts(nc, x, src, dst, edge_weight, W, b, Wr, br, W1, b1, g1, be1, m1, v1,
                W2, b2, g2, be2, m2, v2, Wo, bo, out):
    xn_table = nc.dram_tensor("xn_table", [N, D], F32).ap()

    with ExitStack() as ctx:
        def sb(name, shape, dt=F32):
            return ctx.enter_context(nc.sbuf_tensor(name, shape, dt))

        def sem(name):
            return ctx.enter_context(nc.semaphore(name))

        with ExitStack() as early:
            xbuf = early.enter_context(nc.sbuf_tensor("xbuf", [P, XB, XN * D], F32))
            dstrows = early.enter_context(nc.sbuf_tensor("dstrows", [P, COLS], I32))
            below = early.enter_context(nc.sbuf_tensor("below", [P, COLS], F32))
            dst_raw = early.enter_context(nc.sbuf_tensor("dst_raw", [P, TILES * C], I32))
            src_raw = early.enter_context(nc.sbuf_tensor("src_raw", [P, TILES * C], I32))
            tile_base = early.enter_context(nc.sbuf_tensor("tile_base", [P, TILES * C], F32))
            node_i = early.enter_context(nc.sbuf_tensor("node_i", [P, NT], I32))
            thr_i = early.enter_context(nc.sbuf_tensor("thr_i", [P, TILES], I32))
            thr_f = early.enter_context(nc.sbuf_tensor("thr_f", [P, TILES], F32))
            thrp_i = early.enter_context(nc.sbuf_tensor("thrp_i", [P, 1], I32))
            row_hit = early.enter_context(nc.sbuf_tensor("row_hit", [P, TILES], F32))
            bn_row = [early.enter_context(nc.sbuf_tensor(f"bn_row{n}", [NPAR * E * KT, P], F32)) for n in (1, 2)]
            bn_col = [early.enter_context(nc.sbuf_tensor(f"bn_col{n}", [P, NPAR * E * KT], F32)) for n in (1, 2)]
        w_hi = [sb(f"w{n}_hi", [P, E, KT, D], F32R) for n in (1, 2, 3)]
        w_lo = [sb(f"w{n}_lo", [P, E, KT, D], F32R) for n in (1, 2, 3)]
        gw_hi = sb("gw_hi", [P, KT, D], F32R)
        gw_lo = sb("gw_lo", [P, KT, D], F32R)
        wr_sb = sb("wr_sb", [P, KT, E])
        wr_hi = sb("wr_hi", [P, KT, E], F32R)
        wr_lo = sb("wr_lo", [P, KT, E], F32R)
        bn_scale = [sb(f"bn_scale{n}", [P, E * KT]) for n in (1, 2)]
        bn_bias = [sb(f"bn_bias{n}", [P, E * KT]) for n in (1, 2)]
        b_row = sb("b_row", [1, D])
        br_row = sb("br_row", [1, E])
        bo_sb = sb("bo_sb", [E, D])
        ones = sb("ones", [P, P])
        ident = sb("ident", [P, P])
        node_f = sb("node_f", [P, NT])
        find = sb("find", [P, 8])
        first_i = sb("first_i", [P, 1], I32)
        row_i = sb("row_i", [P, 1], I32)
        starts = sb("starts", [1, TILES], I32)
        win_src = sb("win_src", [P, TILES, C], I16)
        win_dst = sb("win_dst", [P, TILES, C], I16)
        win_w = sb("win_w", [P, TILES, C])
        idx = sb("idx", [P, GT, C], I32)
        dw = sb("dw", [P, 2, 2, C])
        gath = sb("gath", [P, GR, PC, D])
        hot = sb("hot", [P, SR, PC, NT])
        nat = sb("nat", [P, 4, GT * D])
        h1_hi = sb("h1_hi", [P, KT, GN], F32R)
        h1_lo = sb("h1_lo", [P, KT, GN], F32R)
        h2_hi = sb("h2_hi", [P, KT, GN], F32R)
        h2_lo = sb("h2_lo", [P, KT, GN], F32R)
        x2_hi = sb("x2_hi", [P, KT, GN], F32R)
        x2_lo = sb("x2_lo", [P, KT, GN], F32R)
        agg_hi = sb("agg_hi", [P, KT, GN], F32R)
        agg_lo = sb("agg_lo", [P, KT, GN], F32R)
        x1 = sb("x1", [NT, GT, D])
        stat = sb("stat", [P, XN, 6])
        small = sb("small", [P, 2, 4, XN])
        eps = sb("eps", [P, 2])
        affine = sb("affine", [P, 2, XN * XC])
        probs = sb("probs", [NT, GT, E])
        psmall = sb("psmall", [NT, 2, GT])
        probs_t = sb("probs_t", [E, GT, NT])
        y = nat[0:NT, 0, :].rearrange("p (t d) -> p t d", t=GT)
        h_full = nat[:, 1, :].rearrange("p (k n) -> p k n", k=KT)[:, :, 0:GN]
        xn2 = nat[0:NT, 2, :].rearrange("p (t d) -> p t d", t=GT)
        agg = nat[0:NT, 3, :].rearrange("p (t d) -> p t d", t=GT)

        def ps(name):
            return ctx.enter_context(nc.psum_tensor(name, [P, 512], F32))

        ps_h1 = [ps("ps_h1a"), ps("ps_h1b")]
        ps_h2 = [ps("ps_h2a"), ps("ps_h2b")]
        ps_y = [ps("ps_ya"), ps("ps_yb")]
        ps_agg = ps("ps_agg")
        ps_mix = ps("ps_mix")

        s_small = sem("small_loaded")
        s_first = sem("first_loaded")
        s_const = sem("constants_made")
        s_zero = sem("ident_zeroed")
        s_xin = [sem(f"x_loaded{i}") for i in range(XB)]
        s_var = sem("variances_done")
        s_dev = sem("deviations_done")
        s_stat = sem("chunk_affine_done")
        s_norm = sem("chunk_normed")
        s_xout = [sem(f"xn_stored{i}") for i in range(XB)]
        s_hit = sem("row_hits_done")
        s_rows = sem("rows_counted")
        s_row_i = sem("row_index_done")
        s_dstrows = sem("dst_rows_loaded")
        s_start = sem("start_done")
        s_start_t = sem("start_row_done")
        s_starts = sem("starts_written")
        s_win = sem("windows_loaded")
        s_dstrel = sem("windows_converted")
        s_wraw = [sem(f"weights_loaded{i}") for i in range(2)]
        s_whi = sem("weights_hi_done")
        s_wlo = sem("weights_lo_done")
        s_bnt = sem("bn_transposed")
        s_bnvar = sem("bn_variances_there")
        s_bndev = sem("bn_deviations_done")
        s_bn = sem("bn_folded")
        s_setup = sem("dve_setup_step")
        s_step = sem("dve_step")
        s_idx = sem("indices_staged")
        s_gath = [sem(f"rows_gathered{i}") for i in range(GR)]
        s_go = sem("gather_may_start")
        s_hot = sem("onehot_built")
        s_piece = sem("piece_summed")
        s_aggn = sem("agg_copied")
        s_ta = sem("agg_transposed")
        s_tahi = sem("agg_hi_done")
        s_talo = sem("agg_lo_done")
        s_wp = sem("w_product_done")
        s_x1in = sem("x_tile_loaded")
        s_x1 = sem("x1_done")
        s_ln2 = sem("x1_stats_done")
        s_xn2 = sem("x1_normed")
        s_t2 = sem("xn2_transposed")
        s_x2hi = sem("x2_hi_done")
        s_x2lo = sem("x2_lo_done")
        s_lg = sem("logits_done")
        s_lgs = sem("logits_shifted")
        s_exp = sem("exp_done")
        s_prob = sem("probs_done")
        s_pt = sem("probs_transposed")
        s_pts = sem("probs_t_copied")
        s_bo = sem("bo_product_done")
        s_boy = sem("bo_added")
        s_l1 = sem("layer1_done")
        s_h1 = sem("h1_hi_done")
        s_h1lo = sem("h1_lo_done")
        s_l2 = sem("layer2_done")
        s_h2 = sem("h2_hi_done")
        s_h2lo = sem("h2_lo_done")
        s_l3 = sem("layer3_done")
        s_y = sem("y_added")
        s_out = sem("y_stored")

        BODY_STEPS = 11

        FULL, NO_SECOND, LAST = (True, True, True), (True, False, True), (False, False, False)

        def group_loop(eng, body):
            with eng.Fori(0, G - 2) as g:
                body(g, FULL)
            body(G - 2, NO_SECOND)
            body(G - 1, LAST)

        def has_pieces(parts, s):
            return parts[0] if s < E // 2 else parts[1]

        block = ctx.enter_context(nc.Block())

        @block.sync
        def _(sp):
            sp.dma_start(first_i[0:ROWS, :], dst.rearrange("(r c) -> r c", c=COLS)[:, 0:1],
                         allow_slow_non_contiguous=True).then_inc(s_first, 16)
            x_v = x.rearrange("(p n) d -> p (n d)", p=NT)

            def load_x(c):
                if c >= XB:
                    sp.wait_ge(s_xout[c % XB], 16 * (c // XB))
                sp.dma_start(xbuf[0:NT, c % XB, :], x_v[:, c * XN * D:(c + 1) * XN * D]).then_inc(s_xin[c % XB], 16)

            for c in range(XB):
                load_x(c)
            for n, pars in enumerate(((b1, g1, be1, m1, v1), (b2, g2, be2, m2, v2))):
                for q, par in enumerate(pars):
                    sp.dma_start(bn_row[n][q * E * KT:(q + 1) * E * KT, :],
                                 par.rearrange("e (k p) -> (e k) p", p=P)).then_inc(s_small, 16)
            sp.dma_start(b_row[:], b.unsqueeze(0)).then_inc(s_small, 16)
            sp.dma_start(br_row[:], br.unsqueeze(0)).then_inc(s_small, 16)
            sp.dma_start(wr_sb[:], Wr.rearrange("(k p) e -> p k e", p=P)).then_inc(s_small, 16)
            sp.dma_start(bo_sb[:], bo).then_inc(s_small, 16)
            for c in range(XB, XC):
                load_x(c)
            sp.wait_ge(s_starts, 1)
            with sp.Fori(0, TILES) as t:
                start = sp.value_load(starts[0:1, bass.ds(t, 1)], min_val=0, max_val=NE - WIN)
                sp.dma_start(src_raw[:, bass.ds(t * C, C)],
                             src[bass.ds(start, WIN)].rearrange("(p c) -> p c", c=C)).then_inc(s_win, 16)
                sp.dma_start(dst_raw[:, bass.ds(t * C, C)],
                             dst[bass.ds(start, WIN)].rearrange("(p c) -> p c", c=C)).then_inc(s_win, 16)
                sp.dma_start(win_w[:, bass.ds(t, 1), :].rearrange("p o c -> p (o c)"),
                             edge_weight[bass.ds(start, WIN)].rearrange("(p c) -> p c", c=C)).then_inc(s_win, 16)
            for n in range(13):
                if n >= 2:
                    sp.wait_ge(s_wlo, n - 1)
                if n == 0:
                    sp.dma_start(nat[:, 0, 0:KT * D].rearrange("p (k d) -> p k d", k=KT),
                                 W.rearrange("(k p) d -> p k d", p=P)).then_inc(s_wraw[0], 16)
                    continue
                layer, pair = divmod(n - 1, 4)
                w = (W1, W2, Wo)[layer][2 * pair:2 * pair + 2]
                sp.dma_start(nat[:, n % 2, :].rearrange("p (e k d) -> p e k d", e=2, k=KT),
                             w.rearrange("e (k p) d -> p e k d", p=P)).then_inc(s_wraw[n % 2], 16)

            x_t = x.rearrange("(g t p) d -> g p t d", t=GT, p=NT)
            out_t = out.rearrange("(g t p) d -> g p t d", t=GT, p=NT)

            def load_x1(g):
                sp.dma_start(x1[:], x_t[bass.ds(g, 1)].rearrange("o p t d -> (o p) t d")).then_inc(s_x1in, 16)

            load_x1(0)

            def body(g, parts):
                if parts[2]:
                    sp.wait_ge(s_y, GT * E * g + GT)
                    load_x1(g + 1)
                sp.wait_ge(s_y, GT * E * g + GT * E)
                sp.dma_start(out_t[bass.ds(g, 1)].rearrange("o p t d -> (o p) t d"), y).then_inc(s_out, 16)

            group_loop(sp, body)
            sp.wait_ge(s_out, 16 * G)

        @block.gpsimd
        def _(pool):
            nc.gpsimd.iota(node_i[:], pattern=[[1, NT]], base=0, channel_multiplier=0)
            nc.gpsimd.iota(thr_i[:], pattern=[[NT, TILES]], base=0, channel_multiplier=0)
            nc.gpsimd.iota(thrp_i[:], pattern=[[0, 1]], base=0, channel_multiplier=NT)
            nc.gpsimd.iota(tile_base[:].rearrange("p (t c) -> p t c", c=C), pattern=[[NT, TILES], [0, C]],
                           base=0, channel_multiplier=0, allow_small_or_imprecise_dtypes=True)
            nc.gpsimd.memset(ones[:], 1.0)
            nc.gpsimd.memset(eps[:, 0:1], LN_EPS)
            nc.gpsimd.memset(eps[:, 1:2], BN_EPS)
            nc.gpsimd.memset(ident[:], 0.0).then_inc(s_zero, 1)
            pool.wait_ge(s_zero, 1)
            nc.gpsimd.affine_select(out=ident[:], in_=ident[:], compare_op=ALU.not_equal, fill=1.0, base=0,
                                    pattern=[[-1, P]], channel_multiplier=1).then_inc(s_const, 1)
            pool.wait_ge(s_row_i, 1)
            pool.indirect_dma_start(out=dstrows[0:TILES, :], out_offset=None,
                                    in_=dst.rearrange("(r c) -> r c", c=COLS),
                                    in_offset=bass.IndirectOffsetOnAxis(ap=row_i[0:TILES, :], axis=0),
                                    ).then_inc(s_dstrows, 16)
            for i in range(XB):
                pool.wait_ge(s_xout[i], 16 * len(range(i, XC, XB)))

            def gather(g, r, first=False):
                tile, u = r // PT, r % PT
                if u == 0:
                    pool.wait_ge(s_idx, GT * g + tile + 1)
                if not (first and r < GR):
                    pool.wait_ge(s_piece, PG * g + r - GR + 1)
                pool.sem_inc(s_go, 1)
                for c in range(PC):
                    pool.indirect_dma_start(out=gath[:, r % GR, c, :], out_offset=None, in_=xn_table,
                                            in_offset=bass.IndirectOffsetOnAxis(
                                                ap=idx[:, tile, u * PC + c:u * PC + c + 1], axis=0),
                                            ).then_inc(s_gath[r % GR], 16)

            for r in range(PG):
                gather(0, r, first=True)
            with pool.Fori(1, G) as g:
                for r in range(PG):
                    gather(g, r)

        @block.scalar
        def _(act):
            xn_v = xn_table.rearrange("(p n) d -> p (n d)", p=NT)
            def deviations(n, half, wanted):
                act.wait_ge(s_var, wanted)
                nc.scalar.activation(small[0:NT, half, 3, 0:n], small[0:NT, half, 2, 0:n], ACT.Sqrt,
                                     bias=eps[0:NT, 0:1]).then_inc(s_dev, 1)

            deviations(XN, 0, 1)
            for c in range(XC):
                if c + 1 < XC:
                    deviations(XN, (c + 1) % 2, c + 2)
                act.wait_ge(s_stat, c + 1)
                for n in range(XN):
                    j = c * XN + n
                    last = nc.scalar.activation(xbuf[0:NT, c % XB, n * D:(n + 1) * D],
                                                xbuf[0:NT, c % XB, n * D:(n + 1) * D], ACT.Identity,
                                                bias=affine[0:NT, 1, j:j + 1], scale=affine[0:NT, 0, j:j + 1])
                last.then_inc(s_norm, 1)
                act.wait_ge(s_norm, c + 1)
                act.dma_start(xn_v[:, c * XN * D:(c + 1) * XN * D], xbuf[0:NT, c % XB, :]).then_inc(s_xout[c % XB], 16)
            for n in range(2):
                act.wait_ge(s_bnvar, n + 1)
                vv = bn_col[n][:, (NPAR - 1) * E * KT:]
                nc.scalar.activation(vv, vv, ACT.Sqrt, bias=eps[:, 1:2]).then_inc(s_bndev, 1)
            act.wait_ge(s_bn, 1)
            for i in range(XB):
                act.wait_ge(s_xout[i], 16 * len(range(i, XC, XB)))
            act.wait_ge(s_dstrel, 1)

            def weights_hi(n):
                act.wait_ge(s_wraw[n % 2], 16 * (n // 2 + 1))
                if n == 0:
                    nc.scalar.copy(gw_hi[:].rearrange("p k d -> p (k d)"), nat[:, 0, 0:KT * D]).then_inc(s_whi, 1)
                    return
                layer, pair = divmod(n - 1, 4)
                nc.scalar.copy(w_hi[layer][:, 2 * pair:2 * pair + 2].rearrange("p e k d -> p (e k d)"),
                               nat[:, n % 2, :]).then_inc(s_whi, 1)

            def copy_agg(tile, i):
                act.wait_ge(s_piece, PT * tile + PT)
                nc.scalar.copy(agg[:, i, :], ps_agg[0:NT, i % 2 * D:(i % 2 + 1) * D]).then_inc(s_aggn, 1)

            def split_hi(g, done, hi, out_sem, k):
                act.wait_ge(done, KT * g + k + 1)
                nc.scalar.copy(hi[:, k, :], ps_mix[:, 0:GN]).then_inc(out_sem, 1)

            def norm(g):
                act.wait_ge(s_ln2, g + 1)
                if not (isinstance(g, int) and g == 0):
                    act.wait_ge(s_t2, KT * g)
                for i in range(GT):
                    last = nc.scalar.activation(xn2[:, i, :], x1[:, i, :], ACT.Identity,
                                                bias=affine[0:NT, 1, i:i + 1], scale=affine[0:NT, 0, i:i + 1])
                last.then_inc(s_xn2, 1)

            for i in range(GT):
                for n in range(3 * i, 3 * i + 3):
                    weights_hi(n)
                copy_agg(i, i)
            for k in range(KT):
                split_hi(0, s_ta, agg_hi, s_tahi, k)
            weights_hi(12)
            copy_agg(GT, 0)
            deviations(GT, 0, XC + 1)
            norm(0)
            copy_agg(GT + 1, 1)
            for k in range(KT):
                split_hi(0, s_t2, x2_hi, s_x2hi, k)

            def hidden(g, s, layer, first):
                done, ps_in, hi, hi_done, lo_done, freed = (
                    (s_l1, ps_h1, h1_hi, s_h1, s_h1lo, s_l2), (s_l2, ps_h2, h2_hi, s_h2, s_h2lo, s_l3))[layer]
                for k in range(KT):
                    act.wait_ge(done, KT * (E * g + s) + k + 1)
                    if layer == 1:
                        act.wait_ge(s_h1lo, KT * (E * g + s) + k + 1)
                    elif not (first and s == 0):
                        act.wait_ge(s_h2lo, KT * (E * g + s - 1) + k + 1)
                    col = s * KT + k
                    nc.scalar.activation(h_full[:, k, :], ps_in[k][:, 0:GN], ACT.Relu,
                                         bias=bn_bias[layer][:, col:col + 1], scale=bn_scale[layer][:, col:col + 1])
                    if k == 0 and not (first and s == 0):
                        if layer == 0:
                            act.wait_ge(s_l2, KT * (E * g + s))
                        else:
                            act.wait_ge(s_l3, GT * (E * g + s))
                    nc.scalar.activation(hi[:, k, :], ps_in[k][:, 0:GN], ACT.Relu,
                                         bias=bn_bias[layer][:, col:col + 1],
                                         scale=bn_scale[layer][:, col:col + 1]).then_inc(hi_done, 1)

            def body(g, parts, first=False):
                def copy_done(s):
                    if has_pieces(parts, s) and s % 2 == 1:
                        i = (s // 2 + 2) % GT
                        if i == 0:
                            act.wait_ge(s_ta, KT * g + 2 * KT)
                        copy_agg(GT * g + GT + 2 + s // 2, i)

                for s in range(E):
                    hidden(g, s, 0, first)
                    if s < E - 1:
                        copy_done(s)
                    if s == 0:
                        act.wait_ge(s_lgs, g + 1)
                        nc.scalar.activation(probs[:], probs[:], ACT.Exp).then_inc(s_exp, 1)
                    if parts[2] and s == 4:
                        for k in range(KT):
                            split_hi(g + 1, s_ta, agg_hi, s_tahi, k)
                    if parts[2] and s == 5:
                        deviations(GT, 0, g + XC + 2)
                    if parts[2] and s == 6:
                        norm(g + 1)
                    if parts[2] and s == 7:
                        for k in range(KT):
                            split_hi(g + 1, s_t2, x2_hi, s_x2hi, k)
                    hidden(g, s, 1, first)
                copy_done(E - 1)

            body(0, FULL, first=True)
            with act.Fori(1, G - 2) as g:
                body(g, FULL)
            body(G - 2, NO_SECOND)
            body(G - 1, LAST)

        @block.vector
        def _(dve):
            steps = [0]

            def setup(ins):
                ins.then_inc(s_setup, 1)
                steps[0] += 1
                dve.wait_ge(s_setup, steps[0])

            v = nc.vector
            dve.wait_ge(s_const, 1)
            setup(v.tensor_copy(node_f[:], node_i[:]))
            setup(v.tensor_copy(thr_f[:], thr_i[:]))
            dve.wait_ge(s_first, 16)
            setup(v.tensor_copy(find[0:ROWS, 0:1], first_i[0:ROWS, :]))
            v.tensor_scalar(row_hit[0:ROWS, :], thr_f[0:ROWS, :], find[0:ROWS, 0:1], None,
                            ALU.is_gt).then_inc(s_hit, 1)
            dve.wait_ge(s_rows, 1)
            setup(v.tensor_scalar(find[0:TILES, 1:2], ps_mix[0:TILES, 0:1], -1.0, 0.0, ALU.add, ALU.max))
            v.tensor_copy(row_i[0:TILES, :], find[0:TILES, 1:2]).then_inc(s_row_i, 1)
            setup(v.tensor_copy(find[0:TILES, 2:3], thrp_i[0:TILES, :]))

            def layer_norm_stats(n, half, src_of, link):
                for m in range(n):
                    last = v.bn_stats(stat[0:NT, m, :], src_of(m))
                link(last)
                st = stat[0:NT, 0:n, :]
                sm = [small[0:NT, half, q, 0:n] for q in range(4)]
                v.tensor_tensor(sm[0], st[:, :, 1], st[:, :, 4], ALU.add)
                v.tensor_tensor(sm[1], st[:, :, 1], st[:, :, 4], ALU.subtract)
                link(v.tensor_tensor(sm[2], st[:, :, 2], st[:, :, 5], ALU.add))
                link(v.scalar_tensor_tensor(sm[3], sm[1], 0.25, sm[1], ALU.mult, ALU.mult))
                return v.scalar_tensor_tensor(sm[2], sm[2], 1.0 / D, sm[3], ALU.mult, ALU.add)

            def layer_norm_affine(n, half, j, link):
                sm = [small[0:NT, half, q, 0:n] for q in range(4)]
                link(v.reciprocal(affine[0:NT, 0, j:j + n], sm[3]))
                return v.scalar_tensor_tensor(affine[0:NT, 1, j:j + n], sm[0], -0.5, affine[0:NT, 0, j:j + n],
                                              ALU.mult, ALU.mult)

            for c in range(XC + 1):
                if c < XC:
                    dve.wait_ge(s_xin[c % XB], 16 * (c // XB + 1))
                    layer_norm_stats(XN, c % 2, lambda m: xbuf[0:NT, c % XB, m * D:(m + 1) * D],
                                     setup).then_inc(s_var, 1)
                if c > 0:
                    dve.wait_ge(s_dev, c)
                    layer_norm_affine(XN, (c - 1) % 2, (c - 1) * XN, setup).then_inc(s_stat, 1)
                if c == 4:
                    dve.wait_ge(s_dstrows, 16)
                    setup(v.tensor_scalar(below[0:TILES, :], dstrows[0:TILES, :], find[0:TILES, 2:3], None, ALU.is_lt))
                    setup(v.tensor_reduce(find[0:TILES, 3:4], below[0:TILES, :], AX_X, ALU.add))
                    setup(v.scalar_tensor_tensor(find[0:TILES, 4:5], find[0:TILES, 1:2], float(COLS),
                                                 find[0:TILES, 3:4], ALU.mult, ALU.add))
                    v.tensor_scalar(find[0:TILES, 5:6], find[0:TILES, 4:5], float(NE - WIN), None,
                                    ALU.min).then_inc(s_start, 1)
                    dve.wait_ge(s_start_t, 1)
                    v.tensor_copy(starts[:], ps_mix[0:1, 0:TILES]).then_inc(s_starts, 1)
            dve.wait_ge(s_bnt, 1)
            for n in range(2):
                v.tensor_copy(bn_col[n][:], ps_mix[:, n * D:n * D + NPAR * E * KT]).then_inc(s_bnvar, 1)
                bb, gg, be, mm, vv = (bn_col[n][:, q * E * KT:(q + 1) * E * KT] for q in range(NPAR))
                dve.wait_ge(s_bndev, n + 1)
                setup(v.reciprocal(vv, vv))
                setup(v.tensor_tensor(bn_scale[n][:], gg, vv, ALU.mult))
                setup(v.tensor_tensor(bb, bb, mm, ALU.subtract))
                setup(v.tensor_tensor(bb, bb, bn_scale[n][:], ALU.mult))
                last = v.tensor_tensor(bn_bias[n][:], bb, be, ALU.add)
            last.then_inc(s_bn, 1)
            setup(v.tensor_copy(wr_hi[:], wr_sb[:]))
            setup(v.tensor_tensor(wr_lo[:], wr_sb[:], wr_hi[:].bitcast(F32), ALU.subtract))
            dve.wait_ge(s_win, 16 * 3 * TILES)
            v.tensor_copy(win_src[:].rearrange("p t c -> p (t c)"), src_raw[:])
            v.tensor_tensor(win_dst[:].rearrange("p t c -> p (t c)"), dst_raw[:], tile_base[:],
                            ALU.subtract).then_inc(s_dstrel, 1)
            dve.wait_ge(s_dstrel, 1)

            def stage_indices(tile, i):
                v.tensor_copy(idx[:, i, :], win_src[:, bass.ds(tile, 1), :].rearrange("p o c -> p (o c)")
                              ).then_inc(s_idx, 1)

            def stage(tile, i):
                v.tensor_copy(dw[:, i % 2, 0, :], win_dst[:, bass.ds(tile, 1), :].rearrange("p o c -> p (o c)"))
                return v.tensor_copy(dw[:, i % 2, 1, :],
                                     win_w[:, bass.ds(tile, 1), :].rearrange("p o c -> p (o c)"))

            def onehot(q, r):
                i, u = r // PT % 2, r % PT
                dve.wait_ge(s_piece, q - SR + 1) if not (isinstance(q, int) and q < SR) else None
                for c in range(PC):
                    k = u * PC + c
                    last = v.tensor_scalar(hot[:, r % SR, c, :], node_f[:], dw[:, i, 0, k:k + 1],
                                           dw[:, i, 1, k:k + 1], ALU.is_equal, ALU.mult)
                last.then_inc(s_hot, 1)

            def lo_half(lo, whole, hi, lo_done):
                v.tensor_tensor(lo, whole, hi.bitcast(F32), ALU.subtract).then_inc(lo_done, 1)

            def add_x1(g, i):
                dve.wait_ge(s_wp, 2 * g + i + 1)
                v.tensor_tensor(x1[:, 2 * i:2 * i + 2, :], ps_mix[0:NT, :].rearrange("p (t d) -> p t d", t=2),
                                x1[:, 2 * i:2 * i + 2, :], ALU.add).then_inc(s_x1, 1)

            weights_left = list(range(13))

            def split_weights():
                n = weights_left.pop(0)
                dve.wait_ge(s_whi, n + 1)
                if n == 0:
                    lo_half(gw_lo[:].rearrange("p k d -> p (k d)"), nat[:, 0, 0:KT * D],
                            gw_hi[:].rearrange("p k d -> p (k d)"), s_wlo)
                    return
                layer, pair = divmod(n - 1, 4)
                lo_half(w_lo[layer][:, 2 * pair:2 * pair + 2].rearrange("p e k d -> p (e k d)"), nat[:, n % 2, :],
                        w_hi[layer][:, 2 * pair:2 * pair + 2].rearrange("p e k d -> p (e k d)"), s_wlo)

            for tile in range(AHEAD):
                stage_indices(tile, tile % GT)

            def pieces(tiles):
                for tile in tiles:
                    stage_indices(tile + AHEAD, (tile + AHEAD) % GT)
                    setup(stage(tile, tile % GT))
                    for u in range(PT):
                        onehot(tile * PT + u, tile * PT + u)
                        if weights_left and u < 3:
                            split_weights()

            pieces(range(GT))
            for k in range(KT):
                dve.wait_ge(s_tahi, k + 1)
                lo_half(agg_lo[:, k, :], ps_mix[:, 0:GN], agg_hi[:, k, :], s_talo)
            pieces(range(GT, GT + 1))
            dve.wait_ge(s_x1in, 16)
            for i in range(2):
                add_x1(0, i)
            dve.wait_ge(s_x1, 2)
            layer_norm_stats(GT, 0, lambda m: x1[:, m, :], setup).then_inc(s_var, 1)
            dve.wait_ge(s_dev, XC + 1)
            layer_norm_affine(GT, 0, 0, setup).then_inc(s_ln2, 1)
            pieces(range(GT + 1, GT + 2))
            for k in range(KT):
                dve.wait_ge(s_x2hi, k + 1)
                lo_half(x2_lo[:, k, :], ps_mix[:, 0:GN], x2_hi[:, k, :], s_x2lo)

            def body(g, parts, base, first=False):
                done = [0]

                def link(ins):
                    ins.then_inc(s_step, 1)
                    done[0] += 1
                    dve.wait_ge(s_step, base + done[0])

                def hidden_lo(s, layer):
                    hi, lo, hi_done, lo_done = ((h1_hi, h1_lo, s_h1, s_h1lo), (h2_hi, h2_lo, s_h2, s_h2lo))[layer]
                    for k in range(KT):
                        dve.wait_ge(hi_done, KT * (E * g + s) + k + 1)
                        lo_half(lo[:, k, :], h_full[:, k, :], hi[:, k, :], lo_done)

                def add_y(e):
                    if e == 0:
                        if not first:
                            dve.wait_ge(s_out, 16 * g)
                    for i in range(GT):
                        dve.wait_ge(s_l3, GT * (E * g + e) + i + 1)
                        into = x1[:, i, :] if e == 0 else y[:, i, :]
                        v.scalar_tensor_tensor(y[:, i, :], ps_y[i % 2][0:NT, i // 2 * D:(i // 2 + 1) * D],
                                               probs[:, i, e:e + 1], into, ALU.mult, ALU.add).then_inc(s_y, 1)

                def softmax_shift():
                    dve.wait_ge(s_lg, g + 1)
                    logits = ps_mix[0:NT, 0:GT * E].rearrange("p (t e) -> p t e", e=E)
                    link(v.tensor_reduce(psmall[:, 0, :], logits, AX_X, ALU.max))
                    v.tensor_tensor(probs[:], logits, psmall[:, 0, :].unsqueeze(2).broadcast_to([NT, GT, E]),
                                    ALU.subtract).then_inc(s_lgs, 1)

                def softmax_scale():
                    dve.wait_ge(s_exp, g + 1)
                    link(v.tensor_reduce(psmall[:, 1, :], probs[:], AX_X, ALU.add))
                    link(v.reciprocal(psmall[:, 1, :], psmall[:, 1, :]))
                    v.tensor_tensor(probs[:], probs[:], psmall[:, 1, :].unsqueeze(2).broadcast_to([NT, GT, E]),
                                    ALU.mult).then_inc(s_prob, 1)

                def add_bo(i):
                    dve.wait_ge(s_bo, 2 * g + i + 1)
                    if i == 0:
                        dve.wait_ge(s_y, GT * E * g + 2 * GT)
                    v.tensor_tensor(y[:, 2 * i:2 * i + 2, :], ps_mix[0:NT, :].rearrange("p (t d) -> p t d", t=2),
                                    y[:, 2 * i:2 * i + 2, :], ALU.add).then_inc(s_boy, 1)

                for s in range(E):
                    hidden_lo(s, 0)
                    if has_pieces(parts, s):
                        if s % 2 == 0 and parts == FULL:
                            stage_indices(GT * g + GT + 2 + AHEAD + s // 2, (2 + AHEAD + s // 2) % GT)
                        if s % 2 == 0:
                            link(stage(GT * g + GT + 2 + s // 2, (s // 2 + 2) % GT))
                        for u in range(PS):
                            onehot(PG * g + LEAD + PS * s + u, LEAD + PS * s + u)
                    if s == 0:
                        softmax_shift()
                        softmax_scale()
                    if s > 0:
                        add_y(s - 1)
                    if s == 1:
                        dve.wait_ge(s_pt, g + 1)
                        v.tensor_copy(probs_t[:].rearrange("e t n -> e (t n)"), ps_mix[0:E, 0:GN]).then_inc(s_pts, 1)
                    if s == 2:
                        for i in range(2):
                            add_bo(i)
                        dve.wait_ge(s_boy, 2 * g + 2)
                    if parts[2] and s == 4:
                        for k in range(KT):
                            dve.wait_ge(s_tahi, KT * g + KT + k + 1)
                            lo_half(agg_lo[:, k, :], ps_mix[:, 0:GN], agg_hi[:, k, :], s_talo)
                    if parts[2] and s == 5:
                        dve.wait_ge(s_x1in, 16 * g + 32)
                        for i in range(2):
                            add_x1(g + 1, i)
                        dve.wait_ge(s_x1, 2 * g + 4)
                        layer_norm_stats(GT, 0, lambda m: x1[:, m, :], link).then_inc(s_var, 1)
                        dve.wait_ge(s_dev, g + XC + 2)
                        layer_norm_affine(GT, 0, 0, link).then_inc(s_ln2, 1)
                    if parts[2] and s == 7:
                        for k in range(KT):
                            dve.wait_ge(s_x2hi, KT * g + KT + k + 1)
                            lo_half(x2_lo[:, k, :], ps_mix[:, 0:GN], x2_hi[:, k, :], s_x2lo)
                    hidden_lo(s, 1)
                add_y(E - 1)
                if parts == FULL:
                    assert done[0] == BODY_STEPS, done
                return done[0]

            body(0, FULL, 0, first=True)
            with dve.Fori(1, G - 2) as g:
                body(g, FULL, g * BODY_STEPS)
            n = body(G - 2, NO_SECOND, (G - 2) * BODY_STEPS)
            body(G - 1, LAST, (G - 2) * BODY_STEPS + n)

        @block.tensor
        def _(pe):
            mm = nc.tensor.matmul

            pe.wait_ge(s_hit, 1)
            mm(ps_mix[0:TILES, 0:1], row_hit[0:ROWS, :], ones[0:ROWS, 0:1], start=True, stop=True).then_inc(s_rows, 1)
            pe.wait_ge(s_start, 1)
            mm(ps_mix[0:1, 0:TILES], find[0:TILES, 5:6], ident[0:TILES, 0:TILES],
               start=True, stop=True).then_inc(s_start_t, 1)
            n_small = 2 * NPAR + 4
            pe.wait_ge(s_small, 16 * n_small)
            pe.wait_ge(s_starts, 1)
            rows = NPAR * E * KT
            for n in range(2):
                last = mm(ps_mix[:, n * D:n * D + rows], bn_row[n][:], ident[0:rows, 0:rows], start=True, stop=True)
            last.then_inc(s_bnt, 1)
            pe.wait_ge(s_bn, 1)

            def product(out, hi_l, lo_l, hi_r, lo_r, start=True, stop=True):
                mm(out, hi_l, hi_r, start=start, stop=False)
                mm(out, hi_l, lo_r, start=False, stop=False)
                return mm(out, lo_l, hi_r, start=False, stop=stop)

            def sum_piece(q, r, gathered):
                tile, u = r // PT, r % PT
                pe.wait_ge(s_gath[r % GR], gathered)
                pe.wait_ge(s_hot, q + 1)
                for c in range(PC):
                    last = mm(ps_agg[0:NT, tile % 2 * D:(tile % 2 + 1) * D], hot[:, r % SR, c, :],
                              gath[:, r % GR, c, :], start=(u == 0 and c == 0), stop=(u == PT - 1 and c == PC - 1))
                last.then_inc(s_piece, 1)

            def transpose_block(src_of, k, done):
                for i in range(GT):
                    last = nc.tensor.transpose(ps_mix[:, i * NT:(i + 1) * NT], src_of[:, i, k * P:(k + 1) * P],
                                               ident[0:NT, 0:NT])
                last.then_inc(done, 1)

            def w_product(i):
                for t in range(2):
                    tile = slice((2 * i + t) * NT, (2 * i + t + 1) * NT)
                    o = ps_mix[0:NT, t * D:(t + 1) * D]
                    mm(o, ones[0:1, 0:NT], b_row[:], start=True, stop=False)
                    for k in range(KT):
                        last = product(o, agg_hi[:, k, tile], agg_lo[:, k, tile], gw_hi[:, k, :], gw_lo[:, k, :],
                                       start=False, stop=k == KT - 1)
                last.then_inc(s_wp, 1)

            def gathered_count(g, r):
                return 16 * PC * (PG // GR) * g + 16 * PC * (r // GR + 1)

            for r in range(PG):
                if r >= PT and r % PT == 0:
                    pe.wait_ge(s_aggn, r // PT)
                sum_piece(r, r, gathered_count(0, r))
            pe.wait_ge(s_aggn, GT)
            transpose_block(agg, 0, s_ta)
            pe.wait_ge(s_talo, 1)
            transpose_block(agg, 1, s_ta)
            for r in range(PG, PG + PT):
                sum_piece(r, r, gathered_count(0, r))
            pe.wait_ge(s_talo, 2)
            pe.wait_ge(s_wlo, 1)
            w_product(0)
            pe.wait_ge(s_x1, 1)
            w_product(1)
            pe.wait_ge(s_aggn, GT + 1)
            for r in range(PG + PT, LEAD):
                sum_piece(r, r, gathered_count(0, r))
            pe.wait_ge(s_xn2, 1)
            transpose_block(xn2, 0, s_t2)
            pe.wait_ge(s_x2lo, 1)
            transpose_block(xn2, 1, s_t2)
            pe.wait_ge(s_wlo, 13)

            def body(g, parts, first=False):
                def layer(s, n):
                    ps_o, hi, lo, done = ((ps_h1, x2_hi, x2_lo, s_l1), (ps_h2, h1_hi, h1_lo, s_l2))[n]
                    if n == 0 and s == 0:
                        pe.wait_ge(s_x2lo, KT * g + KT)
                    if n == 1:
                        pe.wait_ge(s_h1lo, KT * (E * g + s) + KT)
                    if n == 0 and not (first and s == 0):
                        pe.wait_ge(s_h1, KT * (E * g + s))
                    if n == 1 and not (first and s == 0):
                        pe.wait_ge(s_h2, KT * (E * g + s))
                    for m in range(KT):
                        for k in range(KT):
                            cols = slice(m * P, (m + 1) * P)
                            last = product(ps_o[m][:, 0:GN], w_hi[n][:, s, k, cols], w_lo[n][:, s, k, cols],
                                           hi[:, k, :], lo[:, k, :], start=k == 0, stop=k == KT - 1)
                        last.then_inc(done, 1)

                def output(e):
                    pe.wait_ge(s_h2lo, KT * (E * g + e) + KT)
                    for i in range(GT):
                        if not (first and e == 0 and i < 2):
                            pe.wait_ge(s_y, GT * (E * g + e) + i - 1)
                        o = ps_y[i % 2][0:NT, i // 2 * D:(i // 2 + 1) * D]
                        tile = slice(i * NT, (i + 1) * NT)
                        for k in range(KT):
                            last = product(o, h2_hi[:, k, tile], h2_lo[:, k, tile], w_hi[2][:, e, k, :],
                                           w_lo[2][:, e, k, :], start=k == 0, stop=k == KT - 1)
                        last.then_inc(s_l3, 1)

                def sums(s):
                    if has_pieces(parts, s):
                        if s % 2 == 0:
                            pe.wait_ge(s_aggn, GT * g + GT + s // 2 + 2)
                        for u in range(PS):
                            r = LEAD + PS * s + u
                            sum_piece(PG * g + r, r, gathered_count(g, r))

                def logits():
                    for i in range(GT):
                        o = ps_mix[0:NT, i * E:(i + 1) * E]
                        tile = slice(i * NT, (i + 1) * NT)
                        mm(o, ones[0:1, 0:NT], br_row[:], start=True, stop=False)
                        for k in range(KT):
                            last = product(o, x2_hi[:, k, tile], x2_lo[:, k, tile], wr_hi[:, k, :], wr_lo[:, k, :],
                                           start=False, stop=k == KT - 1)
                    last.then_inc(s_lg, 1)

                def bo_product(i):
                    for t in range(2):
                        last = mm(ps_mix[0:NT, t * D:(t + 1) * D], probs_t[:, 2 * i + t, :], bo_sb[:],
                                  start=True, stop=True)
                    last.then_inc(s_bo, 1)

                for s in range(E):
                    layer(s, 0)
                    if s < E - 1:
                        sums(s)
                    if s == 0:
                        logits()
                    if s == 1:
                        pe.wait_ge(s_prob, g + 1)
                        for i in range(GT):
                            last = nc.tensor.transpose(ps_mix[0:E, i * NT:(i + 1) * NT], probs[:, i, :],
                                                       ident[0:NT, 0:NT])
                        last.then_inc(s_pt, 1)
                    if s == 2:
                        pe.wait_ge(s_pts, g + 1)
                        bo_product(0)
                    if parts[2] and s == 4:
                        pe.wait_ge(s_aggn, GT * g + 2 * GT)
                        transpose_block(agg, 0, s_ta)
                    if parts[2] and s == 5:
                        pe.wait_ge(s_talo, KT * g + 2 * KT)
                        w_product(0)
                    if parts[2] and s == 7:
                        pe.wait_ge(s_xn2, g + 2)
                        transpose_block(xn2, 0, s_t2)
                    if s > 0:
                        output(s - 1)
                    if s == 2:
                        pe.wait_ge(s_boy, 2 * g + 1)
                        bo_product(1)
                    if parts[2] and s == 4:
                        pe.wait_ge(s_talo, KT * g + KT + 1)
                        transpose_block(agg, 1, s_ta)
                    if parts[2] and s == 5:
                        pe.wait_ge(s_x1, 2 * g + 3)
                        w_product(1)
                    if parts[2] and s == 7:
                        pe.wait_ge(s_x2lo, KT * g + KT + 1)
                        transpose_block(xn2, 1, s_t2)
                    layer(s, 1)
                sums(E - 1)
                output(E - 1)

            body(0, FULL, first=True)
            with pe.Fori(1, G - 2) as g:
                body(g, FULL)
            body(G - 2, NO_SECOND)
            body(G - 1, LAST)


_INS = ["x", "src", "dst", "edge_weight", "L0_gnn_W", "L0_gnn_b", "L0_ffn_Wr", "L0_ffn_br", "L0_ffn_W1", "L0_ffn_b1",
        "L0_ffn_g1", "L0_ffn_be1", "L0_ffn_m1", "L0_ffn_v1", "L0_ffn_W2", "L0_ffn_b2", "L0_ffn_g2", "L0_ffn_be2",
        "L0_ffn_m2", "L0_ffn_v2", "L0_ffn_Wo", "L0_ffn_bo"]


def kernel(**inputs):
    import numpy as _np
    import concourse.bacc as _bacc
    from concourse import mybir as _mybir
    from concourse.bass_utils import run_bass_kernel_spmd as _run

    nc = _bacc.Bacc("TRN2", target_bir_lowering=False, num_devices=1)
    arrays, args = {}, []
    for name in _INS:
        a = _np.ascontiguousarray(inputs[name])
        arrays[f"in_{name}"] = a
        args.append(nc.dram_tensor(f"in_{name}", a.shape, _mybir.dt.from_np(a.dtype), kind="ExternalInput").ap())
    args.append(nc.dram_tensor("out_x", (N, D), F32, kind="ExternalOutput").ap())
    gnn_experts(nc, *args)
    r = _run(nc, [arrays], core_ids=[0])
    return r.results[0]["out_x"]
```

```python
from contextlib import ExitStack

import concourse.bass as bass
from concourse import mybir

F32 = mybir.dt.float32
F32R = mybir.dt.float32r
I32 = mybir.dt.int32
ALU = mybir.AluOpType
ACT = mybir.ActivationFunctionType
AX_X = mybir.AxisListType.X

P = 128
D = 256
KT = D // P
E = 8
N = 12500
NE = 212500
NT = 125
TILES = N // NT
GT = 4
GN = GT * NT
G = TILES // GT
C = 18
WIN = C * P
PC = 3
PT = C // PC
PG = PT * GT
PS = PG // E
GR = 8
SR = 4
AHEAD = 2
LEAD = PG + PG // 2
ROWS = 125
COLS = NE // ROWS
XN = 5
XC = N // NT // XN
XB = 8
LN_EPS = 1e-5
BN_EPS = 1e-3
NPAR = 5


def gnn_experts(nc, x, src, dst, edge_weight, W, b, Wr, br, W1, b1, g1, be1, m1, v1,
                W2, b2, g2, be2, m2, v2, Wo, bo, out):
    xn_table = nc.dram_tensor("xn_table", [N, D], F32).ap()

    with ExitStack() as ctx:
        def sb(name, shape, dt=F32):
            return ctx.enter_context(nc.sbuf_tensor(name, shape, dt))

        def sem(name):
            return ctx.enter_context(nc.semaphore(name))

        with ExitStack() as early:
            xbuf = early.enter_context(nc.sbuf_tensor("xbuf", [P, XB, XN * D], F32))
            dstrows = early.enter_context(nc.sbuf_tensor("dstrows", [P, COLS], I32))
            below = early.enter_context(nc.sbuf_tensor("below", [P, COLS], F32))
            node_i = early.enter_context(nc.sbuf_tensor("node_i", [P, NT], I32))
            thr_i = early.enter_context(nc.sbuf_tensor("thr_i", [P, TILES], I32))
            thrp_i = early.enter_context(nc.sbuf_tensor("thrp_i", [P, 1], I32))
            row_hit = early.enter_context(nc.sbuf_tensor("row_hit", [P, TILES], F32))
            bn_row = [early.enter_context(nc.sbuf_tensor(f"bn_row{n}", [NPAR * E * KT, P], F32)) for n in (1, 2)]
            bn_col = [early.enter_context(nc.sbuf_tensor(f"bn_col{n}", [P, NPAR * E * KT], F32)) for n in (1, 2)]
        w_hi = [sb(f"w{n}_hi", [P, E, KT, D], F32R) for n in (1, 2, 3)]
        w_lo = [sb(f"w{n}_lo", [P, E, KT, D], F32R) for n in (1, 2, 3)]
        gw_hi = sb("gw_hi", [P, KT, D], F32R)
        gw_lo = sb("gw_lo", [P, KT, D], F32R)
        wr_sb = sb("wr_sb", [P, KT, E])
        wr_pair = sb("wr_pair", [P, KT, 2, E], F32R)
        bn_scale = [sb(f"bn_scale{n}", [P, E * KT]) for n in (1, 2)]
        bn_bias = [sb(f"bn_bias{n}", [P, E * KT]) for n in (1, 2)]
        b_row = sb("b_row", [1, D])
        b_half = sb("b_half", [1, 2, D], F32R)
        b_pair = sb("b_pair", [2, D], F32R)
        br_all = sb("br_all", [NT, E])
        bo_sb = sb("bo_sb", [E, D])
        bo_half = sb("bo_half", [E, 2, D], F32R)
        bo_three = sb("bo_three", [3 * E, D], F32R)
        ones = sb("ones", [P, P])
        ones_r = sb("ones_r", [2, NT], F32R)
        ident = sb("ident", [P, P])
        node_f = sb("node_f", [P, NT])
        find = sb("find", [P, 8])
        first_i = sb("first_i", [P, 1], I32)
        row_i = sb("row_i", [P, 1], I32)
        starts = sb("starts", [1, TILES], I32)
        thr_f = sb("thr_f", [P, TILES])
        idx = sb("idx", [P, GT, C], I32)
        win_dst = sb("win_dst", [P, GT, C], I32)
        win_w = sb("win_w", [P, GT, C])
        rel = sb("rel", [P, GT, C])
        gath = sb("gath", [P, GR, PC, D])
        hot = sb("hot", [P, SR, PC, NT])
        nat = sb("nat", [P, 4, GT * D])
        h1_hi = sb("h1_hi", [P, KT, GN], F32R)
        h1_lo = sb("h1_lo", [P, KT, GN], F32R)
        h2_hi = sb("h2_hi", [P, KT, GN], F32R)
        h2_lo = sb("h2_lo", [P, KT, GN], F32R)
        x2_hi = sb("x2_hi", [P, KT, GN], F32R)
        x2_lo = sb("x2_lo", [P, KT, GN], F32R)
        agg_hi = sb("agg_hi", [P, KT, GN], F32R)
        agg_lo = sb("agg_lo", [P, KT, GN], F32R)
        x1 = sb("x1", [NT, GT, D])
        stat = sb("stat", [P, XN, 6])
        small = sb("small", [P, 2, 4, XN])
        eps = sb("eps", [P, 2])
        affine = sb("affine", [P, 2, XN * XC])
        probs = sb("probs", [NT, GT, E])
        psmall = sb("psmall", [NT, 2, GT])
        probs_hi = sb("probs_hi", [NT, GT, E], F32R)
        probs_three = sb("probs_three", [NT, GT, 3, E])
        probs_t = sb("probs_t", [3 * E, GT, NT], F32R)
        y = nat[0:NT, 0, :].rearrange("p (t d) -> p t d", t=GT)
        h_full = nat[:, 1, :].rearrange("p (k n) -> p k n", k=KT)[:, :, 0:GN]
        xn2 = nat[0:NT, 2, :].rearrange("p (t d) -> p t d", t=GT)
        agg = nat[0:NT, 3, :].rearrange("p (t d) -> p t d", t=GT)

        def ps(name):
            return ctx.enter_context(nc.psum_tensor(name, [P, 512], F32))

        ps_h1 = [ps("ps_h1a"), ps("ps_h1b")]
        ps_h2 = [ps("ps_h2a"), ps("ps_h2b")]
        ps_y = [ps("ps_ya"), ps("ps_yb")]
        ps_agg = ps("ps_agg")
        ps_mix = ps("ps_mix")

        s_small = sem("small_loaded")
        s_first = sem("first_loaded")
        s_const = sem("constants_made")
        s_zero = sem("ident_zeroed")
        s_xin = [sem(f"x_loaded{i}") for i in range(XB)]
        s_var = sem("variances_done")
        s_dev = sem("deviations_done")
        s_stat = sem("chunk_affine_done")
        s_norm = sem("chunk_normed")
        s_xout = [sem(f"xn_stored{i}") for i in range(XB)]
        s_hit = sem("row_hits_done")
        s_rows = sem("rows_counted")
        s_row_i = sem("row_index_done")
        s_dstrows = sem("dst_rows_loaded")
        s_start = sem("start_done")
        s_start_t = sem("start_row_done")
        s_starts = sem("starts_written")
        s_win = [sem(f"window_loaded{i}") for i in range(GT)]
        s_wraw = [sem(f"weights_loaded{i}") for i in range(2)]
        s_whi = sem("weights_hi_done")
        s_wlo = sem("weights_lo_done")
        s_bnt = sem("bn_transposed")
        s_bnvar = sem("bn_variances_there")
        s_bndev = sem("bn_deviations_done")
        s_bn = sem("bn_folded")
        s_halves = sem("b_bo_split")
        s_stacked = sem("b_bo_stacked")
        s_setup = sem("dve_setup_step")
        s_step = sem("dve_step")
        s_gath = [sem(f"rows_gathered{i}") for i in range(GR)]
        s_go = sem("gather_may_start")
        s_hot = sem("onehot_built")
        s_piece = sem("piece_summed")
        s_aggn = sem("agg_copied")
        s_ta = sem("agg_transposed")
        s_tahi = sem("agg_hi_done")
        s_talo = sem("agg_lo_done")
        s_wp = sem("w_product_done")
        s_x1in = sem("x_tile_loaded")
        s_x1 = sem("x1_done")
        s_ln2 = sem("x1_stats_done")
        s_xn2 = sem("x1_normed")
        s_t2 = sem("xn2_transposed")
        s_x2hi = sem("x2_hi_done")
        s_x2lo = sem("x2_lo_done")
        s_lg = sem("logits_done")
        s_lgs = sem("logits_shifted")
        s_exp = sem("exp_done")
        s_prob = sem("probs_done")
        s_pt = sem("probs_transposed")
        s_pts = sem("probs_t_copied")
        s_bo = sem("bo_product_done")
        s_boy = sem("bo_added")
        s_l1 = sem("layer1_done")
        s_h1 = sem("h1_hi_done")
        s_h1lo = sem("h1_lo_done")
        s_l2 = sem("layer2_done")
        s_h2 = sem("h2_hi_done")
        s_h2lo = sem("h2_lo_done")
        s_l3 = sem("layer3_done")
        s_y = sem("y_added")
        s_out = sem("y_stored")

        BODY_STEPS = 15

        FULL, NO_SECOND, LAST = (True, True, True), (True, False, True), (False, False, False)

        def group_loop(eng, body):
            with eng.Fori(0, G - 2) as g:
                body(g, FULL)
            body(G - 2, NO_SECOND)
            body(G - 1, LAST)

        def has_pieces(parts, s):
            return parts[0] if s < E // 2 else parts[1]

        block = ctx.enter_context(nc.Block())

        @block.sync
        def _(sp):
            sp.dma_start(first_i[0:ROWS, :], dst.rearrange("(r c) -> r c", c=COLS)[:, 0:1],
                         allow_slow_non_contiguous=True).then_inc(s_first, 16)
            x_v = x.rearrange("(p n) d -> p (n d)", p=NT)

            def load_x(c):
                if c >= XB:
                    sp.wait_ge(s_xout[c % XB], 16 * (c // XB))
                sp.dma_start(xbuf[0:NT, c % XB, :], x_v[:, c * XN * D:(c + 1) * XN * D]).then_inc(s_xin[c % XB], 16)

            for c in range(XB):
                load_x(c)
            for n, pars in enumerate(((b1, g1, be1, m1, v1), (b2, g2, be2, m2, v2))):
                for q, par in enumerate(pars):
                    sp.dma_start(bn_row[n][q * E * KT:(q + 1) * E * KT, :],
                                 par.rearrange("e (k p) -> (e k) p", p=P)).then_inc(s_small, 16)
            sp.dma_start(b_row[:], b.unsqueeze(0)).then_inc(s_small, 16)
            sp.dma_start(br_all[:], br.unsqueeze(0).broadcast_to([NT, E])).then_inc(s_small, 16)
            sp.dma_start(wr_sb[:], Wr.rearrange("(k p) e -> p k e", p=P)).then_inc(s_small, 16)
            sp.dma_start(bo_sb[:], bo).then_inc(s_small, 16)
            for c in range(XB, XC):
                load_x(c)
            sp.wait_ge(s_halves, 1)
            for to, of in ((b_pair[0:1, :], b_half[:, 0, :]), (b_pair[1:2, :], b_half[:, 1, :]),
                           (bo_three[0:E, :], bo_half[:, 0, :]), (bo_three[E:2 * E, :], bo_half[:, 0, :]),
                           (bo_three[2 * E:3 * E, :], bo_half[:, 1, :])):
                sp.dma_start(to.bitcast(F32), of.bitcast(F32)).then_inc(s_stacked, 16)

            def load_window(tile, i):
                start = sp.value_load(starts[0:1, bass.ds(tile, 1)], min_val=0, max_val=NE - WIN)
                for to, of in ((idx, src), (win_dst, dst), (win_w, edge_weight)):
                    sp.dma_start(to[:, i, :], of[bass.ds(start, WIN)].rearrange("(p c) -> p c", c=C)
                                 ).then_inc(s_win[i], 16)

            sp.wait_ge(s_starts, 1)
            for tile in range(GT):
                load_window(tile, tile)
            for n in range(13):
                if n >= 2:
                    sp.wait_ge(s_wlo, n - 1)
                if n == 0:
                    sp.dma_start(nat[:, 0, 0:KT * D].rearrange("p (k d) -> p k d", k=KT),
                                 W.rearrange("(k p) d -> p k d", p=P)).then_inc(s_wraw[0], 16)
                    continue
                layer, pair = divmod(n - 1, 4)
                w = (W1, W2, Wo)[layer][2 * pair:2 * pair + 2]
                sp.dma_start(nat[:, n % 2, :].rearrange("p (e k d) -> p e k d", e=2, k=KT),
                             w.rearrange("e (k p) d -> p e k d", p=P)).then_inc(s_wraw[n % 2], 16)

            x_t = x.rearrange("(g t p) d -> g p t d", t=GT, p=NT)
            out_t = out.rearrange("(g t p) d -> g p t d", t=GT, p=NT)

            def load_x1(g):
                sp.dma_start(x1[:], x_t[bass.ds(g, 1)].rearrange("o p t d -> (o p) t d")).then_inc(s_x1in, 16)

            load_x1(0)
            for tile in range(GT, GT + 2 + AHEAD):
                sp.wait_ge(s_piece, PT * (tile - GT + 1))
                load_window(tile, tile % GT)

            def body(g, parts):
                for s in range(0, E, 2):
                    if parts == FULL:
                        tile = 2 + AHEAD + s // 2
                        sp.wait_ge(s_piece, PT * GT * g + PT * (tile + 1))
                        load_window(GT * g + GT + tile, tile % GT)
                    if parts[2] and s == 2:
                        sp.wait_ge(s_y, GT * E * g + GT)
                        load_x1(g + 1)
                sp.wait_ge(s_y, GT * E * g + GT * E)
                sp.dma_start(out_t[bass.ds(g, 1)].rearrange("o p t d -> (o p) t d"), y).then_inc(s_out, 16)

            group_loop(sp, body)
            sp.wait_ge(s_out, 16 * G)

        @block.gpsimd
        def _(pool):
            nc.gpsimd.iota(node_i[:], pattern=[[1, NT]], base=0, channel_multiplier=0)
            nc.gpsimd.iota(thr_i[:], pattern=[[NT, TILES]], base=0, channel_multiplier=0)
            nc.gpsimd.iota(thrp_i[:], pattern=[[0, 1]], base=0, channel_multiplier=NT)
            nc.gpsimd.memset(ones[:], 1.0)
            nc.gpsimd.memset(eps[:, 0:1], LN_EPS)
            nc.gpsimd.memset(eps[:, 1:2], BN_EPS)
            nc.gpsimd.memset(ident[:], 0.0).then_inc(s_zero, 1)
            pool.wait_ge(s_zero, 1)
            nc.gpsimd.affine_select(out=ident[:], in_=ident[:], compare_op=ALU.not_equal, fill=1.0, base=0,
                                    pattern=[[-1, P]], channel_multiplier=1).then_inc(s_const, 1)
            pool.wait_ge(s_row_i, 1)
            pool.indirect_dma_start(out=dstrows[0:TILES, :], out_offset=None,
                                    in_=dst.rearrange("(r c) -> r c", c=COLS),
                                    in_offset=bass.IndirectOffsetOnAxis(ap=row_i[0:TILES, :], axis=0),
                                    ).then_inc(s_dstrows, 16)
            for i in range(XB):
                pool.wait_ge(s_xout[i], 16 * len(range(i, XC, XB)))

            def gather(g, r, first=False):
                tile, u = r // PT, r % PT
                if u == 0:
                    pool.wait_ge(s_win[tile], 48 * g + 48)
                if not (first and r < GR):
                    pool.wait_ge(s_piece, PG * g + r - GR + 1)
                pool.sem_inc(s_go, 1)
                for c in range(PC):
                    pool.indirect_dma_start(out=gath[:, r % GR, c, :], out_offset=None, in_=xn_table,
                                            in_offset=bass.IndirectOffsetOnAxis(
                                                ap=idx[:, tile, u * PC + c:u * PC + c + 1], axis=0),
                                            ).then_inc(s_gath[r % GR], 16)

            for r in range(PG):
                gather(0, r, first=True)
            with pool.Fori(1, G) as g:
                for r in range(PG):
                    gather(g, r)

        @block.scalar
        def _(act):
            xn_v = xn_table.rearrange("(p n) d -> p (n d)", p=NT)
            def deviations(n, half, wanted):
                act.wait_ge(s_var, wanted)
                nc.scalar.activation(small[0:NT, half, 3, 0:n], small[0:NT, half, 2, 0:n], ACT.Sqrt,
                                     bias=eps[0:NT, 0:1]).then_inc(s_dev, 1)

            deviations(XN, 0, 1)
            for c in range(XC):
                if c + 1 < XC:
                    deviations(XN, (c + 1) % 2, c + 2)
                act.wait_ge(s_stat, c + 1)
                for n in range(XN):
                    j = c * XN + n
                    last = nc.scalar.activation(xbuf[0:NT, c % XB, n * D:(n + 1) * D],
                                                xbuf[0:NT, c % XB, n * D:(n + 1) * D], ACT.Identity,
                                                bias=affine[0:NT, 1, j:j + 1], scale=affine[0:NT, 0, j:j + 1])
                last.then_inc(s_norm, 1)
                act.wait_ge(s_norm, c + 1)
                act.dma_start(xn_v[:, c * XN * D:(c + 1) * XN * D], xbuf[0:NT, c % XB, :]).then_inc(s_xout[c % XB], 16)
            for n in range(2):
                act.wait_ge(s_bnvar, n + 1)
                vv = bn_col[n][:, (NPAR - 1) * E * KT:]
                nc.scalar.activation(vv, vv, ACT.Sqrt, bias=eps[:, 1:2]).then_inc(s_bndev, 1)
            act.wait_ge(s_bn, 1)
            for i in range(XB):
                act.wait_ge(s_xout[i], 16 * len(range(i, XC, XB)))

            def weights_hi(n):
                act.wait_ge(s_wraw[n % 2], 16 * (n // 2 + 1))
                if n == 0:
                    nc.scalar.copy(gw_hi[:].rearrange("p k d -> p (k d)"), nat[:, 0, 0:KT * D]).then_inc(s_whi, 1)
                    return
                layer, pair = divmod(n - 1, 4)
                nc.scalar.copy(w_hi[layer][:, 2 * pair:2 * pair + 2].rearrange("p e k d -> p (e k d)"),
                               nat[:, n % 2, :]).then_inc(s_whi, 1)

            def copy_agg(tile, i):
                act.wait_ge(s_piece, PT * tile + PT)
                nc.scalar.copy(agg[:, i, :], ps_agg[0:NT, i % 2 * D:(i % 2 + 1) * D]).then_inc(s_aggn, 1)

            def split_hi(g, done, hi, out_sem, k):
                act.wait_ge(done, KT * g + k + 1)
                nc.scalar.copy(hi[:, k, :], ps_mix[:, 0:GN]).then_inc(out_sem, 1)

            def norm(g):
                act.wait_ge(s_ln2, g + 1)
                if not (isinstance(g, int) and g == 0):
                    act.wait_ge(s_t2, KT * g)
                for i in range(GT):
                    last = nc.scalar.activation(xn2[:, i, :], x1[:, i, :], ACT.Identity,
                                                bias=affine[0:NT, 1, i:i + 1], scale=affine[0:NT, 0, i:i + 1])
                last.then_inc(s_xn2, 1)

            for i in range(GT):
                for n in range(3 * i, 3 * i + 3):
                    weights_hi(n)
                copy_agg(i, i)
            for k in range(KT):
                split_hi(0, s_ta, agg_hi, s_tahi, k)
            weights_hi(12)
            copy_agg(GT, 0)
            deviations(GT, 0, XC + 1)
            norm(0)
            copy_agg(GT + 1, 1)
            for k in range(KT):
                split_hi(0, s_t2, x2_hi, s_x2hi, k)

            def hidden(g, s, layer, first):
                done, ps_in, hi, hi_done, lo_done, freed = (
                    (s_l1, ps_h1, h1_hi, s_h1, s_h1lo, s_l2), (s_l2, ps_h2, h2_hi, s_h2, s_h2lo, s_l3))[layer]
                for k in range(KT):
                    act.wait_ge(done, KT * (E * g + s) + k + 1)
                    if layer == 1:
                        act.wait_ge(s_h1lo, KT * (E * g + s) + k + 1)
                    elif not (first and s == 0):
                        act.wait_ge(s_h2lo, KT * (E * g + s - 1) + k + 1)
                    col = s * KT + k
                    nc.scalar.activation(h_full[:, k, :], ps_in[k][:, 0:GN], ACT.Relu,
                                         bias=bn_bias[layer][:, col:col + 1], scale=bn_scale[layer][:, col:col + 1])
                    if k == 0 and not (first and s == 0):
                        if layer == 0:
                            act.wait_ge(s_l2, KT * (E * g + s))
                        else:
                            act.wait_ge(s_l3, GT * (E * g + s))
                    nc.scalar.activation(hi[:, k, :], ps_in[k][:, 0:GN], ACT.Relu,
                                         bias=bn_bias[layer][:, col:col + 1],
                                         scale=bn_scale[layer][:, col:col + 1]).then_inc(hi_done, 1)

            def body(g, parts, first=False):
                def copy_done(s):
                    if has_pieces(parts, s) and s % 2 == 1:
                        i = (s // 2 + 2) % GT
                        if i == 0:
                            act.wait_ge(s_ta, KT * g + 2 * KT)
                        copy_agg(GT * g + GT + 2 + s // 2, i)

                for s in range(E):
                    hidden(g, s, 0, first)
                    if s < E - 1:
                        copy_done(s)
                    if s == 0:
                        act.wait_ge(s_lgs, g + 1)
                        nc.scalar.activation(probs[:], probs[:], ACT.Exp).then_inc(s_exp, 1)
                    if parts[2] and s == 4:
                        for k in range(KT):
                            split_hi(g + 1, s_ta, agg_hi, s_tahi, k)
                    if parts[2] and s == 6:
                        deviations(GT, 0, g + XC + 2)
                    if parts[2] and s == 7:
                        for k in range(KT):
                            split_hi(g + 1, s_t2, x2_hi, s_x2hi, k)
                    hidden(g, s, 1, first)
                    if parts[2] and s == 6:
                        norm(g + 1)
                copy_done(E - 1)

            body(0, FULL, first=True)
            with act.Fori(1, G - 2) as g:
                body(g, FULL)
            body(G - 2, NO_SECOND)
            body(G - 1, LAST)

        @block.vector
        def _(dve):
            steps = [0]

            def setup(ins):
                ins.then_inc(s_setup, 1)
                steps[0] += 1
                dve.wait_ge(s_setup, steps[0])

            v = nc.vector
            dve.wait_ge(s_const, 1)
            setup(v.tensor_copy(node_f[:], node_i[:]))
            setup(v.tensor_copy(thr_f[:], thr_i[:]))
            dve.wait_ge(s_first, 16)
            setup(v.tensor_copy(find[0:ROWS, 0:1], first_i[0:ROWS, :]))
            v.tensor_scalar(row_hit[0:ROWS, :], thr_f[0:ROWS, :], find[0:ROWS, 0:1], None,
                            ALU.is_gt).then_inc(s_hit, 1)
            dve.wait_ge(s_rows, 1)
            setup(v.tensor_scalar(find[0:TILES, 1:2], ps_mix[0:TILES, 0:1], -1.0, 0.0, ALU.add, ALU.max))
            v.tensor_copy(row_i[0:TILES, :], find[0:TILES, 1:2]).then_inc(s_row_i, 1)
            setup(v.tensor_copy(find[0:TILES, 2:3], thrp_i[0:TILES, :]))

            def layer_norm_stats(n, half, src_of, link):
                for m in range(n):
                    last = v.bn_stats(stat[0:NT, m, :], src_of(m))
                link(last)
                st = stat[0:NT, 0:n, :]
                sm = [small[0:NT, half, q, 0:n] for q in range(4)]
                v.tensor_tensor(sm[0], st[:, :, 1], st[:, :, 4], ALU.add)
                v.tensor_tensor(sm[1], st[:, :, 1], st[:, :, 4], ALU.subtract)
                link(v.tensor_tensor(sm[2], st[:, :, 2], st[:, :, 5], ALU.add))
                link(v.scalar_tensor_tensor(sm[3], sm[1], 0.25, sm[1], ALU.mult, ALU.mult))
                return v.scalar_tensor_tensor(sm[2], sm[2], 1.0 / D, sm[3], ALU.mult, ALU.add)

            def layer_norm_affine(n, half, j, link):
                sm = [small[0:NT, half, q, 0:n] for q in range(4)]
                link(v.reciprocal(affine[0:NT, 0, j:j + n], sm[3]))
                return v.scalar_tensor_tensor(affine[0:NT, 1, j:j + n], sm[0], -0.5, affine[0:NT, 0, j:j + n],
                                              ALU.mult, ALU.mult)

            for c in range(XC + 1):
                if c < XC:
                    dve.wait_ge(s_xin[c % XB], 16 * (c // XB + 1))
                    layer_norm_stats(XN, c % 2, lambda m: xbuf[0:NT, c % XB, m * D:(m + 1) * D],
                                     setup).then_inc(s_var, 1)
                if c > 0:
                    dve.wait_ge(s_dev, c)
                    layer_norm_affine(XN, (c - 1) % 2, (c - 1) * XN, setup).then_inc(s_stat, 1)
                if c == 4:
                    dve.wait_ge(s_dstrows, 16)
                    setup(v.tensor_scalar(below[0:TILES, :], dstrows[0:TILES, :], find[0:TILES, 2:3], None, ALU.is_lt))
                    setup(v.tensor_reduce(find[0:TILES, 3:4], below[0:TILES, :], AX_X, ALU.add))
                    setup(v.scalar_tensor_tensor(find[0:TILES, 4:5], find[0:TILES, 1:2], float(COLS),
                                                 find[0:TILES, 3:4], ALU.mult, ALU.add))
                    v.tensor_scalar(find[0:TILES, 5:6], find[0:TILES, 4:5], float(NE - WIN), None,
                                    ALU.min).then_inc(s_start, 1)
                    dve.wait_ge(s_start_t, 1)
                    v.tensor_copy(starts[:], ps_mix[0:1, 0:TILES]).then_inc(s_starts, 1)
            dve.wait_ge(s_bnt, 1)
            for n in range(2):
                v.tensor_copy(bn_col[n][:], ps_mix[:, n * D:n * D + NPAR * E * KT]).then_inc(s_bnvar, 1)
                bb, gg, be, mm, vv = (bn_col[n][:, q * E * KT:(q + 1) * E * KT] for q in range(NPAR))
                dve.wait_ge(s_bndev, n + 1)
                setup(v.reciprocal(vv, vv))
                setup(v.tensor_tensor(bn_scale[n][:], gg, vv, ALU.mult))
                setup(v.tensor_tensor(bb, bb, mm, ALU.subtract))
                setup(v.tensor_tensor(bb, bb, bn_scale[n][:], ALU.mult))
                last = v.tensor_tensor(bn_bias[n][:], bb, be, ALU.add)
            last.then_inc(s_bn, 1)
            v.tensor_copy(ones_r[:], ones[0:2, 0:NT])
            v.tensor_copy(b_half[:, 0, :], b_row[:])
            v.tensor_copy(bo_half[:, 0, :], bo_sb[:])
            setup(v.tensor_copy(wr_pair[:, :, 0, :], wr_sb[:]))
            v.tensor_tensor(b_half[:, 1, :], b_row[:], b_half[:, 0, :].bitcast(F32), ALU.subtract)
            v.tensor_tensor(bo_half[:, 1, :], bo_sb[:], bo_half[:, 0, :].bitcast(F32), ALU.subtract)
            setup(v.tensor_tensor(wr_pair[:, :, 1, :], wr_sb[:], wr_pair[:, :, 0, :].bitcast(F32), ALU.subtract))
            v.tensor_copy(find[0:1, 6:7], find[0:1, 5:6]).then_inc(s_halves, 1)
            def stage(g, tile, i):
                dve.wait_ge(s_win[i], 48 * g + 48)
                return v.tensor_scalar(rel[:, i, :], win_dst[:, i, :], thr_f[:, bass.ds(tile, 1)], None, ALU.subtract)

            def onehot(q, r):
                i, u = r // PT % GT, r % PT
                dve.wait_ge(s_piece, q - SR + 1) if not (isinstance(q, int) and q < SR) else None
                for c in range(PC):
                    k = u * PC + c
                    last = v.tensor_scalar(hot[:, r % SR, c, :], node_f[:], rel[:, i, k:k + 1],
                                           win_w[:, i, k:k + 1], ALU.is_equal, ALU.mult)
                last.then_inc(s_hot, 1)

            def lo_half(lo, whole, hi, lo_done):
                v.tensor_tensor(lo, whole, hi.bitcast(F32), ALU.subtract).then_inc(lo_done, 1)

            def add_x1(g, i):
                dve.wait_ge(s_wp, 2 * g + i + 1)
                v.tensor_tensor(x1[:, 2 * i:2 * i + 2, :], ps_mix[0:NT, :].rearrange("p (t d) -> p t d", t=2),
                                x1[:, 2 * i:2 * i + 2, :], ALU.add).then_inc(s_x1, 1)

            weights_left = list(range(13))

            def split_weights():
                n = weights_left.pop(0)
                dve.wait_ge(s_whi, n + 1)
                if n == 0:
                    lo_half(gw_lo[:].rearrange("p k d -> p (k d)"), nat[:, 0, 0:KT * D],
                            gw_hi[:].rearrange("p k d -> p (k d)"), s_wlo)
                    return
                layer, pair = divmod(n - 1, 4)
                lo_half(w_lo[layer][:, 2 * pair:2 * pair + 2].rearrange("p e k d -> p (e k d)"), nat[:, n % 2, :],
                        w_hi[layer][:, 2 * pair:2 * pair + 2].rearrange("p e k d -> p (e k d)"), s_wlo)

            def pieces(tiles):
                for tile in tiles:
                    setup(stage(tile // GT, tile, tile % GT))
                    for u in range(PT):
                        onehot(tile * PT + u, tile * PT + u)
                        if weights_left and u < 3:
                            split_weights()

            pieces(range(GT))
            for k in range(KT):
                dve.wait_ge(s_tahi, k + 1)
                lo_half(agg_lo[:, k, :], ps_mix[:, 0:GN], agg_hi[:, k, :], s_talo)
            pieces(range(GT, GT + 1))
            dve.wait_ge(s_x1in, 16)
            for i in range(2):
                add_x1(0, i)
            dve.wait_ge(s_x1, 2)
            layer_norm_stats(GT, 0, lambda m: x1[:, m, :], setup).then_inc(s_var, 1)
            dve.wait_ge(s_dev, XC + 1)
            layer_norm_affine(GT, 0, 0, setup).then_inc(s_ln2, 1)
            pieces(range(GT + 1, GT + 2))
            setup(stage(1, GT + 2, 2))
            for q in range(LEAD, LEAD + PS):
                onehot(q, q)
            for k in range(KT):
                dve.wait_ge(s_x2hi, k + 1)
                lo_half(x2_lo[:, k, :], ps_mix[:, 0:GN], x2_hi[:, k, :], s_x2lo)

            def body(g, parts, base, first=False):
                done = [0]

                def link(ins):
                    ins.then_inc(s_step, 1)
                    done[0] += 1
                    dve.wait_ge(s_step, base + done[0])

                def hidden_lo(s, layer):
                    hi, lo, hi_done, lo_done = ((h1_hi, h1_lo, s_h1, s_h1lo), (h2_hi, h2_lo, s_h2, s_h2lo))[layer]
                    for k in range(KT):
                        dve.wait_ge(hi_done, KT * (E * g + s) + k + 1)
                        lo_half(lo[:, k, :], h_full[:, k, :], hi[:, k, :], lo_done)

                def add_y(e):
                    if e == 0:
                        if not first:
                            dve.wait_ge(s_out, 16 * g)
                    for i in range(GT):
                        dve.wait_ge(s_l3, GT * (E * g + e) + i + 1)
                        into = x1[:, i, :] if e == 0 else y[:, i, :]
                        v.scalar_tensor_tensor(y[:, i, :], ps_y[i % 2][0:NT, i // 2 * D:(i // 2 + 1) * D],
                                               probs[:, i, e:e + 1], into, ALU.mult, ALU.add).then_inc(s_y, 1)

                def softmax_shift():
                    dve.wait_ge(s_lg, g + 1)
                    if not first:
                        dve.wait_ge(s_y, GT * E * g)
                    halves = ps_mix[0:NT, 0:GT * 2 * E].rearrange("p (t h e) -> p t h e", h=2, e=E)
                    bias = br_all[:].unsqueeze(1).broadcast_to([NT, GT, E])
                    link(v.tensor_tensor(probs[:], halves[:, :, 0, :], bias, ALU.add))
                    link(v.tensor_tensor(probs[:], halves[:, :, 1, :], probs[:], ALU.add))
                    link(v.tensor_reduce(psmall[:, 0, :], probs[:], AX_X, ALU.max))
                    v.tensor_tensor(probs[:], probs[:], psmall[:, 0, :].unsqueeze(2).broadcast_to([NT, GT, E]),
                                    ALU.subtract).then_inc(s_lgs, 1)

                def softmax_scale():
                    dve.wait_ge(s_exp, g + 1)
                    link(v.tensor_reduce(psmall[:, 1, :], probs[:], AX_X, ALU.add))
                    link(v.reciprocal(psmall[:, 1, :], psmall[:, 1, :]))
                    link(v.tensor_tensor(probs[:], probs[:], psmall[:, 1, :].unsqueeze(2).broadcast_to([NT, GT, E]),
                                         ALU.mult))
                    link(v.tensor_copy(probs_hi[:], probs[:]))
                    v.tensor_copy(probs_three[:, :, 0, :], probs_hi[:].bitcast(F32))
                    v.tensor_copy(probs_three[:, :, 2, :], probs_hi[:].bitcast(F32))
                    v.tensor_tensor(probs_three[:, :, 1, :], probs[:], probs_hi[:].bitcast(F32),
                                    ALU.subtract).then_inc(s_prob, 1)

                def add_bo(i):
                    dve.wait_ge(s_bo, 2 * g + i + 1)
                    dve.wait_ge(s_y, GT * E * g + (i + 1) * GT)
                    v.tensor_tensor(y[:, 2 * i:2 * i + 2, :], ps_mix[0:NT, :].rearrange("p (t d) -> p t d", t=2),
                                    y[:, 2 * i:2 * i + 2, :], ALU.add).then_inc(s_boy, 1)

                def onehots(s):
                    if s % 2 == 0:
                        tile = 2 + s // 2
                        link(stage(g + 1 + tile // GT, GT * g + GT + tile, tile % GT))
                    for u in range(PS):
                        onehot(PG * g + LEAD + PS * s + u, LEAD + PS * s + u)

                def lo_of_agg(k):
                    dve.wait_ge(s_tahi, KT * g + KT + k + 1)
                    lo_half(agg_lo[:, k, :], ps_mix[:, 0:GN], agg_hi[:, k, :], s_talo)

                def lo_of_x2(k):
                    dve.wait_ge(s_x2hi, KT * g + KT + k + 1)
                    lo_half(x2_lo[:, k, :], ps_mix[:, 0:GN], x2_hi[:, k, :], s_x2lo)

                for s in range(E):
                    hidden_lo(s, 0)
                    if s == 0:
                        softmax_shift()
                        softmax_scale()
                    if s == 2:
                        add_bo(0)
                        dve.wait_ge(s_boy, 2 * g + 1)
                    if parts[2] and s == 4:
                        lo_of_agg(0)
                    if parts[2] and s == 5:
                        dve.wait_ge(s_x1in, 16 * g + 32)
                        add_x1(g + 1, 0)
                    if parts[2] and s == 7:
                        lo_of_x2(0)
                    if s > 0:
                        add_y(s - 1)
                    if s == 1:
                        dve.wait_ge(s_pt, g + 1)
                        v.tensor_copy(probs_t[:].rearrange("e t n -> e (t n)"), ps_mix[0:3 * E, 0:GN]).then_inc(s_pts, 1)
                    if s == 2:
                        add_bo(1)
                        dve.wait_ge(s_boy, 2 * g + 2)
                    if parts[2] and s == 4:
                        lo_of_agg(1)
                    if parts[2] and s == 5:
                        add_x1(g + 1, 1)
                        dve.wait_ge(s_x1, 2 * g + 4)
                        layer_norm_stats(GT, 0, lambda m: x1[:, m, :], link).then_inc(s_var, 1)
                    if parts[2] and s == 6:
                        dve.wait_ge(s_dev, g + XC + 2)
                        layer_norm_affine(GT, 0, 0, link).then_inc(s_ln2, 1)
                    if parts[2] and s == 7:
                        lo_of_x2(1)
                    if s < E - 1 and has_pieces(parts, s + 1):
                        onehots(s + 1)
                    hidden_lo(s, 1)
                if parts == FULL:
                    onehots(E)
                add_y(E - 1)
                if parts == FULL:
                    assert done[0] == BODY_STEPS, done
                return done[0]

            body(0, FULL, 0, first=True)
            with dve.Fori(1, G - 2) as g:
                body(g, FULL, g * BODY_STEPS)
            n = body(G - 2, NO_SECOND, (G - 2) * BODY_STEPS)
            body(G - 1, LAST, (G - 2) * BODY_STEPS + n)

        @block.tensor
        def _(pe):
            mm = nc.tensor.matmul

            pe.wait_ge(s_hit, 1)
            mm(ps_mix[0:TILES, 0:1], row_hit[0:ROWS, :], ones[0:ROWS, 0:1], start=True, stop=True).then_inc(s_rows, 1)
            pe.wait_ge(s_start, 1)
            mm(ps_mix[0:1, 0:TILES], find[0:TILES, 5:6], ident[0:TILES, 0:TILES],
               start=True, stop=True).then_inc(s_start_t, 1)
            n_small = 2 * NPAR + 4
            pe.wait_ge(s_small, 16 * n_small)
            pe.wait_ge(s_starts, 1)
            rows = NPAR * E * KT
            for n in range(2):
                last = mm(ps_mix[:, n * D:n * D + rows], bn_row[n][:], ident[0:rows, 0:rows], start=True, stop=True)
            last.then_inc(s_bnt, 1)
            pe.wait_ge(s_bn, 1)

            def product(out, hi_l, lo_l, hi_r, lo_r, start=True, stop=True):
                mm(out, hi_l, hi_r, start=start, stop=False)
                mm(out, hi_l, lo_r, start=False, stop=False)
                return mm(out, lo_l, hi_r, start=False, stop=stop)

            def sum_piece(q, r, gathered):
                tile, u = r // PT, r % PT
                pe.wait_ge(s_gath[r % GR], gathered)
                pe.wait_ge(s_hot, q + 1)
                for c in range(PC):
                    last = mm(ps_agg[0:NT, tile % 2 * D:(tile % 2 + 1) * D], hot[:, r % SR, c, :],
                              gath[:, r % GR, c, :], start=(u == 0 and c == 0), stop=(u == PT - 1 and c == PC - 1))
                last.then_inc(s_piece, 1)

            def transpose_block(src_of, k, done):
                for i in range(GT):
                    last = nc.tensor.transpose(ps_mix[:, i * NT:(i + 1) * NT], src_of[:, i, k * P:(k + 1) * P],
                                               ident[0:NT, 0:NT])
                last.then_inc(done, 1)

            def w_product(i):
                for t in range(2):
                    tile = slice((2 * i + t) * NT, (2 * i + t + 1) * NT)
                    o = ps_mix[0:NT, t * D:(t + 1) * D]
                    mm(o, ones_r[:], b_pair[:], start=True, stop=False)
                    for k in range(KT):
                        last = product(o, agg_hi[:, k, tile], agg_lo[:, k, tile], gw_hi[:, k, :], gw_lo[:, k, :],
                                       start=False, stop=k == KT - 1)
                last.then_inc(s_wp, 1)

            def gathered_count(g, r):
                return 16 * PC * (PG // GR) * g + 16 * PC * (r // GR + 1)

            for r in range(PG):
                if r >= PT and r % PT == 0:
                    pe.wait_ge(s_aggn, r // PT)
                sum_piece(r, r, gathered_count(0, r))
            pe.wait_ge(s_aggn, GT)
            transpose_block(agg, 0, s_ta)
            pe.wait_ge(s_talo, 1)
            transpose_block(agg, 1, s_ta)
            for r in range(PG, PG + PT):
                sum_piece(r, r, gathered_count(0, r))
            pe.wait_ge(s_talo, 2)
            pe.wait_ge(s_wlo, 1)
            pe.wait_ge(s_stacked, 16 * 5)
            w_product(0)
            pe.wait_ge(s_x1, 1)
            w_product(1)
            pe.wait_ge(s_aggn, GT + 1)
            for r in range(PG + PT, LEAD):
                sum_piece(r, r, gathered_count(0, r))
            pe.wait_ge(s_xn2, 1)
            transpose_block(xn2, 0, s_t2)
            pe.wait_ge(s_x2lo, 1)
            transpose_block(xn2, 1, s_t2)
            pe.wait_ge(s_wlo, 13)

            def body(g, parts, first=False):
                def layer(s, n):
                    ps_o, hi, lo, done = ((ps_h1, x2_hi, x2_lo, s_l1), (ps_h2, h1_hi, h1_lo, s_l2))[n]
                    if n == 0 and s == 0:
                        pe.wait_ge(s_x2lo, KT * g + KT)
                    if n == 1:
                        pe.wait_ge(s_h1lo, KT * (E * g + s) + KT)
                    if n == 0 and not (first and s == 0):
                        pe.wait_ge(s_h1, KT * (E * g + s))
                    if n == 1 and not (first and s == 0):
                        pe.wait_ge(s_h2, KT * (E * g + s))
                    for m in range(KT):
                        for k in range(KT):
                            cols = slice(m * P, (m + 1) * P)
                            last = product(ps_o[m][:, 0:GN], w_hi[n][:, s, k, cols], w_lo[n][:, s, k, cols],
                                           hi[:, k, :], lo[:, k, :], start=k == 0, stop=k == KT - 1)
                        last.then_inc(done, 1)

                def output(e):
                    pe.wait_ge(s_h2lo, KT * (E * g + e) + KT)
                    for i in range(GT):
                        if not (first and e == 0 and i < 2):
                            pe.wait_ge(s_y, GT * (E * g + e) + i - 1)
                        o = ps_y[i % 2][0:NT, i // 2 * D:(i // 2 + 1) * D]
                        tile = slice(i * NT, (i + 1) * NT)
                        for k in range(KT):
                            last = product(o, h2_hi[:, k, tile], h2_lo[:, k, tile], w_hi[2][:, e, k, :],
                                           w_lo[2][:, e, k, :], start=k == 0, stop=k == KT - 1)
                        last.then_inc(s_l3, 1)

                def sums(s):
                    if has_pieces(parts, s):
                        if s % 2 == 0:
                            pe.wait_ge(s_aggn, GT * g + GT + s // 2 + 2)
                        for u in range(PS):
                            r = LEAD + PS * s + u
                            sum_piece(PG * g + r, r, gathered_count(g, r))

                def logits():
                    for i in range(GT):
                        o = ps_mix[0:NT, i * 2 * E:(i + 1) * 2 * E]
                        tile = slice(i * NT, (i + 1) * NT)
                        for k in range(KT):
                            pair = wr_pair[:, k, :, :].rearrange("p h e -> p (h e)")
                            mm(o, x2_hi[:, k, tile], pair, start=k == 0, stop=False)
                            last = mm(o, x2_lo[:, k, tile], pair, start=False, stop=k == KT - 1)
                    last.then_inc(s_lg, 1)

                def bo_product(i):
                    for t in range(2):
                        last = mm(ps_mix[0:NT, t * D:(t + 1) * D], probs_t[:, 2 * i + t, :], bo_three[:],
                                  start=True, stop=True)
                    last.then_inc(s_bo, 1)

                for s in range(E):
                    layer(s, 0)
                    if s < E - 1:
                        sums(s)
                    if s == 0:
                        logits()
                    if s == 1:
                        pe.wait_ge(s_prob, g + 1)
                        for i in range(GT):
                            last = nc.tensor.transpose(ps_mix[0:3 * E, i * NT:(i + 1) * NT],
                                                       probs_three[:, i, :, :].rearrange("p h e -> p (h e)"),
                                                       ident[0:NT, 0:NT])
                        last.then_inc(s_pt, 1)
                    if s == 2:
                        pe.wait_ge(s_pts, g + 1)
                        bo_product(0)
                    if parts[2] and s == 4:
                        pe.wait_ge(s_aggn, GT * g + 2 * GT)
                        transpose_block(agg, 0, s_ta)
                    if parts[2] and s == 5:
                        pe.wait_ge(s_talo, KT * g + 2 * KT)
                        w_product(0)
                    if parts[2] and s == 7:
                        pe.wait_ge(s_xn2, g + 2)
                        transpose_block(xn2, 0, s_t2)
                    if s > 0:
                        output(s - 1)
                    if s == 2:
                        pe.wait_ge(s_boy, 2 * g + 1)
                        bo_product(1)
                    if parts[2] and s == 4:
                        pe.wait_ge(s_talo, KT * g + KT + 1)
                        transpose_block(agg, 1, s_ta)
                    if parts[2] and s == 5:
                        pe.wait_ge(s_x1, 2 * g + 3)
                        w_product(1)
                    if parts[2] and s == 7:
                        pe.wait_ge(s_x2lo, KT * g + KT + 1)
                        transpose_block(xn2, 1, s_t2)
                    layer(s, 1)
                sums(E - 1)
                output(E - 1)

            body(0, FULL, first=True)
            with pe.Fori(1, G - 2) as g:
                body(g, FULL)
            body(G - 2, NO_SECOND)
            body(G - 1, LAST)


_INS = ["x", "src", "dst", "edge_weight", "L0_gnn_W", "L0_gnn_b", "L0_ffn_Wr", "L0_ffn_br", "L0_ffn_W1", "L0_ffn_b1",
        "L0_ffn_g1", "L0_ffn_be1", "L0_ffn_m1", "L0_ffn_v1", "L0_ffn_W2", "L0_ffn_b2", "L0_ffn_g2", "L0_ffn_be2",
        "L0_ffn_m2", "L0_ffn_v2", "L0_ffn_Wo", "L0_ffn_bo"]


def kernel(**inputs):
    import numpy as _np
    import concourse.bacc as _bacc
    from concourse import mybir as _mybir
    from concourse.bass_utils import run_bass_kernel_spmd as _run

    nc = _bacc.Bacc("TRN2", target_bir_lowering=False, num_devices=1)
    arrays, args = {}, []
    for name in _INS:
        a = _np.ascontiguousarray(inputs[name])
        arrays[f"in_{name}"] = a
        args.append(nc.dram_tensor(f"in_{name}", a.shape, _mybir.dt.from_np(a.dtype), kind="ExternalInput").ap())
    args.append(nc.dram_tensor("out_x", (N, D), F32, kind="ExternalOutput").ap())
    gnn_experts(nc, *args)
    r = _run(nc, [arrays], core_ids=[0])
    return r.results[0]["out_x"]
```

```python
from contextlib import ExitStack

import concourse.bass as bass
from concourse import mybir

F32 = mybir.dt.float32
F32R = mybir.dt.float32r
I32 = mybir.dt.int32
ALU = mybir.AluOpType
ACT = mybir.ActivationFunctionType
AX_X = mybir.AxisListType.X

P = 128
D = 256
KT = D // P
E = 8
N = 12500
NE = 212500
NT = 125
TILES = N // NT
GT = 4
GN = GT * NT
G = TILES // GT
C = 18
WIN = C * P
PC = 3
PT = C // PC
PG = PT * GT
PS = PG // E
GR = 6
SR = 3
AHEAD = 2
LEAD = PG + PG // 2
ROWS = 125
COLS = NE // ROWS
SE = 125
SELF = -(-(N - NT + WIN) // P)
XN = 5
XC = N // NT // XN
XB = 8
LN_EPS = 1e-5
BN_EPS = 1e-3
NPAR = 5


def gnn_experts(nc, x, src, dst, edge_weight, W, b, Wr, br, W1, b1, g1, be1, m1, v1,
                W2, b2, g2, be2, m2, v2, Wo, bo, out):
    xn_table = nc.dram_tensor("xn_table", [N, D], F32).ap()
    sum_table = nc.dram_tensor("sum_table", [N + P, D], F32).ap()
    self_src = nc.dram_tensor("self_src", [NE], I32).ap()
    self_dst = nc.dram_tensor("self_dst", [NE], I32).ap()
    self_w = nc.dram_tensor("self_w", [NE], F32).ap()

    with ExitStack() as ctx:
        def sb(name, shape, dt=F32):
            return ctx.enter_context(nc.sbuf_tensor(name, shape, dt))

        def sem(name):
            return ctx.enter_context(nc.semaphore(name))

        with ExitStack() as early:
            xbuf = early.enter_context(nc.sbuf_tensor("xbuf", [P, XB, XN * D], F32))
            dstrows = early.enter_context(nc.sbuf_tensor("dstrows", [P, COLS], I32))
            below = early.enter_context(nc.sbuf_tensor("below", [P, COLS], F32))
            dst_all = early.enter_context(nc.sbuf_tensor("dst_all", [ROWS, COLS], I32))
            next_i = early.enter_context(nc.sbuf_tensor("next_i", [ROWS, 1], I32))
            start_row = early.enter_context(nc.sbuf_tensor("start_row", [1, 2, TILES + 1], F32))
            self_i = early.enter_context(nc.sbuf_tensor("self_i", [P, 2, SELF], I32))
            self_f = early.enter_context(nc.sbuf_tensor("self_f", [P, SELF], F32))
            part_i = early.enter_context(nc.sbuf_tensor("part_i", [P, 1], I32))
            edge_i = early.enter_context(nc.sbuf_tensor("edge_i", [SE, 3], I32))
            edge_w = early.enter_context(nc.sbuf_tensor("edge_w", [SE, 1], F32))
            dst_row = early.enter_context(nc.sbuf_tensor("dst_row", [SE, SE], I32))
            same = early.enter_context(nc.sbuf_tensor("same", [SE, 4, SE], F32))
            edge_f = early.enter_context(nc.sbuf_tensor("edge_f", [SE, 8], F32))
            node_i = early.enter_context(nc.sbuf_tensor("node_i", [P, NT], I32))
            thr_i = early.enter_context(nc.sbuf_tensor("thr_i", [P, TILES], I32))
            thrp_i = early.enter_context(nc.sbuf_tensor("thrp_i", [P, 1], I32))
            row_hit = early.enter_context(nc.sbuf_tensor("row_hit", [P, TILES], F32))
            bn_row = [early.enter_context(nc.sbuf_tensor(f"bn_row{n}", [NPAR * E * KT, P], F32)) for n in (1, 2)]
            bn_col = [early.enter_context(nc.sbuf_tensor(f"bn_col{n}", [P, NPAR * E * KT], F32)) for n in (1, 2)]
        w_hi = [sb(f"w{n}_hi", [P, E, KT, D], F32R) for n in (1, 2, 3)]
        w_lo = [sb(f"w{n}_lo", [P, E, KT, D], F32R) for n in (1, 2, 3)]
        gw_hi = sb("gw_hi", [P, KT, D], F32R)
        gw_lo = sb("gw_lo", [P, KT, D], F32R)
        wr_sb = sb("wr_sb", [P, KT, E])
        wr_pair = sb("wr_pair", [P, KT, 2, E], F32R)
        bn_scale = [sb(f"bn_scale{n}", [P, E * KT]) for n in (1, 2)]
        bn_bias = [sb(f"bn_bias{n}", [P, E * KT]) for n in (1, 2)]
        b_pair = sb("b_pair", [2, D], F32R)
        br_all = sb("br_all", [NT, E])
        bo_three = sb("bo_three", [3 * E, D], F32R)
        ones = sb("ones", [P, P])
        ones_r = sb("ones_r", [2, NT], F32R)
        ident = sb("ident", [P, P])
        node_f = sb("node_f", [P, NT])
        find = sb("find", [P, 12])
        general = sb("general", [1, 1], I32)
        first_i = sb("first_i", [P, 1], I32)
        row_i = sb("row_i", [P, 1], I32)
        starts = sb("starts", [1, TILES], I32)
        thr_f = sb("thr_f", [P, TILES])
        idx = sb("idx", [P, GT, C], I32)
        win_dst = sb("win_dst", [P, GT, C], I32)
        win_w = sb("win_w", [P, GT, C])
        rel = sb("rel", [P, GT, C])
        gath = sb("gath", [P, GR, PC, D])
        hot_r = sb("hot_r", [P, SR, PC, NT], F32R)
        rows_hi = sb("rows_hi", [P, SR, PC, D], F32R)
        rows_lo = sb("rows_lo", [P, SR, PC, D], F32R)
        nat = sb("nat", [P, 4, GT * D])
        with ExitStack() as early:
            hot = early.enter_context(nc.sbuf_tensor("hot", [P, SR, PC, NT], F32))
        h1_hi = sb("h1_hi", [P, KT, GN], F32R)
        h1_lo = sb("h1_lo", [P, KT, GN], F32R)
        h2_hi = sb("h2_hi", [P, KT, GN], F32R)
        h2_lo = sb("h2_lo", [P, KT, GN], F32R)
        x2_hi = sb("x2_hi", [P, KT, GN], F32R)
        x2_lo = sb("x2_lo", [P, KT, GN], F32R)
        agg_hi = sb("agg_hi", [P, KT, GN], F32R)
        agg_lo = sb("agg_lo", [P, KT, GN], F32R)
        x1 = sb("x1", [NT, GT, D])
        stat = sb("stat", [P, XN, 6])
        small = sb("small", [P, 2, 4, XN])
        eps = sb("eps", [P, 2])
        affine = sb("affine", [P, 2, XN * XC])
        probs = sb("probs", [NT, GT, E])
        psmall = sb("psmall", [NT, 2, GT])
        probs_hi = sb("probs_hi", [NT, GT, E], F32R)
        probs_three = sb("probs_three", [NT, GT, 3, E])
        with ExitStack() as early:
            b_row = early.enter_context(nc.sbuf_tensor("b_row", [1, D], F32))
            b_half = early.enter_context(nc.sbuf_tensor("b_half", [1, 2, D], F32R))
            bo_sb = early.enter_context(nc.sbuf_tensor("bo_sb", [E, D], F32))
            bo_half = early.enter_context(nc.sbuf_tensor("bo_half", [E, 2, D], F32R))
        probs_t = sb("probs_t", [3 * E, GT, NT], F32R)
        y = nat[0:NT, 0, :].rearrange("p (t d) -> p t d", t=GT)
        h_full = nat[:, 1, :].rearrange("p (k n) -> p k n", k=KT)[:, :, 0:GN]
        xn2 = nat[0:NT, 2, :].rearrange("p (t d) -> p t d", t=GT)
        agg = nat[0:NT, 3, :].rearrange("p (t d) -> p t d", t=GT)

        def ps(name):
            return ctx.enter_context(nc.psum_tensor(name, [P, 512], F32))

        ps_h1 = [ps("ps_h1a"), ps("ps_h1b")]
        ps_h2 = [ps("ps_h2a"), ps("ps_h2b")]
        ps_y = [ps("ps_ya"), ps("ps_yb")]
        ps_agg = ps("ps_agg")
        ps_mix = ps("ps_mix")

        s_small = sem("small_loaded")
        s_first = sem("first_loaded")
        s_const = sem("constants_made")
        s_zero = sem("ident_zeroed")
        s_xin = [sem(f"x_loaded{i}") for i in range(XB)]
        s_var = sem("variances_done")
        s_dev = sem("deviations_done")
        s_stat = sem("chunk_affine_done")
        s_norm = sem("chunk_normed")
        s_norm_last = sem("chunk_last_rows_normed")
        s_xout = [sem(f"xn_stored{i}") for i in range(XB)]
        s_hit = sem("row_hits_done")
        s_rows = sem("rows_counted")
        s_row_i = sem("row_index_done")
        s_dstrows = sem("dst_rows_loaded")
        s_start = sem("start_done")
        s_start_t = sem("start_row_done")
        s_starts = sem("starts_written")
        s_win = [sem(f"window_loaded{i}") for i in range(GT)]
        s_wraw = [sem(f"weights_loaded{i}") for i in range(2)]
        s_whi = sem("weights_hi_done")
        s_wlo = sem("weights_lo_done")
        s_bnt = sem("bn_transposed")
        s_bnvar = sem("bn_variances_there")
        s_bndev = sem("bn_deviations_done")
        s_bn = sem("bn_folded")
        s_halves = sem("b_bo_split")
        s_stacked = sem("b_bo_stacked")
        s_setup = sem("dve_setup_step")
        s_step = sem("dve_step")
        s_gath = [sem(f"rows_gathered{i}") for i in range(GR)]
        s_go = sem("gather_may_start")
        s_hot = sem("onehot_built")
        s_rhi = sem("rows_hi_done")
        s_rlo = sem("rows_lo_done")
        s_piece = sem("piece_summed")
        s_aggn = sem("agg_copied")
        s_ta = sem("agg_transposed")
        s_tahi = sem("agg_hi_done")
        s_talo = sem("agg_lo_done")
        s_wp = sem("w_product_done")
        s_x1in = sem("x_tile_loaded")
        s_x1 = sem("x1_done")
        s_xn2 = sem("x1_normed")
        s_t2 = sem("xn2_transposed")
        s_x2hi = sem("x2_hi_done")
        s_x2lo = sem("x2_lo_done")
        s_lg = sem("logits_done")
        s_lgs = sem("logits_shifted")
        s_exp = sem("exp_done")
        s_prob = sem("probs_done")
        s_pt = sem("probs_transposed")
        s_pts = sem("probs_t_copied")
        s_bo = sem("bo_product_done")
        s_boy = sem("bo_added")
        s_l1 = sem("layer1_done")
        s_h1 = sem("h1_hi_done")
        s_h1lo = sem("h1_lo_done")
        s_l2 = sem("layer2_done")
        s_h2 = sem("h2_hi_done")
        s_h2lo = sem("h2_lo_done")
        s_l3 = sem("layer3_done")
        s_y = sem("y_added")
        s_out = sem("y_stored")

        BODY_STEPS = 16

        s_flag = sem("path_chosen")
        s_whole = sem("dst_loaded")
        s_gstep = sem("general_dve_step")
        s_gloop = sem("general_loop_step")
        s_gzero = sem("general_zeros_there")
        s_gzeroed = sem("sum_table_zeroed")
        s_gself = sem("self_lists_made")
        s_gstarts = sem("self_starts_written")
        s_gin = sem("general_edges_loaded")
        s_grow = sem("general_rows_gathered")
        s_gsame = sem("general_matrix_built")
        s_gmm = sem("general_product_done")
        s_gsum = sem("general_sums_copied")
        s_gadd = sem("general_sums_added")
        s_gcopy = sem("general_tables_copied")

        FULL, NO_SECOND, LAST = (True, True, True), (True, False, True), (False, False, False)

        def has_pieces(parts, s):
            return parts[0] if s < E // 2 else parts[1]

        def gathered_count(g, r):
            return 16 * PC * (PG // GR) * g + 16 * PC * (r // GR + 1)

        def split_count(g, s, u):
            return PS * (E * g + s) + u + 1

        block = ctx.enter_context(nc.Block())

        @block.sync
        def _(sp):
            sp.dma_start(first_i[0:ROWS, :], dst.rearrange("(r c) -> r c", c=COLS)[:, 0:1],
                         allow_slow_non_contiguous=True).then_inc(s_first, 16)
            x_v = x.rearrange("(p n) d -> p (n d)", p=NT)

            def load_x(c):
                if c >= XB:
                    sp.wait_ge(s_xout[c % XB], 16 * (c // XB))
                sp.dma_start(xbuf[0:NT, c % XB, :], x_v[:, c * XN * D:(c + 1) * XN * D]).then_inc(s_xin[c % XB], 16)

            for c in range(XB):
                load_x(c)
            sp.dma_start(dst_all[:], dst.rearrange("(r c) -> r c", c=COLS)).then_inc(s_whole, 16)
            sp.wait_ge(s_const, 1)
            sp.dma_start(next_i[0:ROWS - 1, :], dst[COLS:NE].rearrange("(r c) -> r c", c=COLS)[:, 0:1],
                         allow_slow_non_contiguous=True).then_inc(s_whole, 16)
            for n, pars in enumerate(((b1, g1, be1, m1, v1), (b2, g2, be2, m2, v2))):
                for q, par in enumerate(pars):
                    sp.dma_start(bn_row[n][q * E * KT:(q + 1) * E * KT, :],
                                 par.rearrange("e (k p) -> (e k) p", p=P)).then_inc(s_small, 16)
            sp.dma_start(b_row[:], b.unsqueeze(0)).then_inc(s_small, 16)
            sp.dma_start(br_all[:], br.unsqueeze(0).broadcast_to([NT, E])).then_inc(s_small, 16)
            sp.dma_start(wr_sb[:], Wr.rearrange("(k p) e -> p k e", p=P)).then_inc(s_small, 16)
            sp.dma_start(bo_sb[:], bo).then_inc(s_small, 16)
            for c in range(XB, XC):
                load_x(c)

            def load_lists(start, i, lists):
                for to, of in zip((idx, win_dst, win_w), lists):
                    sp.dma_start(to[:, i, :], of[bass.ds(start, WIN)].rearrange("(p c) -> p c", c=C)
                                 ).then_inc(s_win[i], 16)

            def start_of(tile):
                return sp.value_load(starts[0:1, bass.ds(tile, 1)], min_val=0, max_val=NE - WIN)

            sp.wait_ge(s_starts, 1)
            sp.wait_ge(s_flag, 1)
            general_sp = sp.value_load(general[0:1, 0:1], min_val=0, max_val=1)
            with sp.If(general_sp < 1):
                for tile in range(GT):
                    load_lists(start_of(tile), tile, (src, dst, edge_weight))
            sp.wait_ge(s_halves, 1)
            for to, of in ((b_pair[0:1, :], b_half[:, 0, :]), (b_pair[1:2, :], b_half[:, 1, :]),
                           (bo_three[0:E, :], bo_half[:, 0, :]), (bo_three[E:2 * E, :], bo_half[:, 0, :]),
                           (bo_three[2 * E:3 * E, :], bo_half[:, 1, :])):
                sp.dma_start(to.bitcast(F32), of.bitcast(F32)).then_inc(s_stacked, 16)

            with sp.If(general_sp > 0):
                sp.wait_ge(s_gzero, 1)
                zeros = gath[0:NT, :, :, :].rearrange("p r c d -> p (r c d)")[:, 0:N // NT // 10 * D]
                for i in range(10):
                    sp.dma_start(sum_table[0:N, :].rearrange("(p n) d -> p (n d)", p=NT)
                                 [:, i * N // NT // 10 * D:(i + 1) * N // NT // 10 * D], zeros).then_inc(s_gzeroed, 16)
                sp.dma_start(sum_table[N:N + P, :], gath[:, 0, 0, :]).then_inc(s_gzeroed, 16)
                sp.wait_ge(s_gself, 2)
                for to, of in ((self_src, self_i[:, 1, :]), (self_dst, self_i[:, 0, :]), (self_w, self_f[:])):
                    sp.dma_start(to[0:P * SELF].rearrange("(p l) -> p l", l=SELF), of).then_inc(s_gcopy, 16)

                def load_edges(first):
                    edges = bass.ds(first, SE)
                    for to, of in ((edge_i[:, 0:1], src), (edge_i[:, 1:2], dst), (edge_w[:], edge_weight)):
                        sp.dma_start(to, of[edges].rearrange("(p o) -> p o", o=1)).then_inc(s_gin, 16)
                    sp.dma_start(dst_row[:], dst[edges].unsqueeze(0).broadcast_to([SE, SE])).then_inc(s_gin, 16)

                load_edges(0)
                with sp.Fori(1, NE // SE) as c:
                    sp.wait_ge(s_gadd, c * 16)
                    load_edges(c * SE)
                sp.wait_ge(s_gadd, NE // SE * 16)
                sp.dma_start(xn_table.rearrange("(a b) d -> a (b d)", b=10),
                             sum_table[0:N, :].rearrange("(a b) d -> a (b d)", b=10)).then_inc(s_gcopy, 16)
                sp.wait_ge(s_gcopy, 16 * 4)
                sp.wait_ge(s_gstarts, 1)
                for tile in range(GT):
                    load_lists(start_of(tile), tile, (self_src, self_dst, self_w))

            def load_window(tile, i):
                start = start_of(tile)
                with sp.If(general_sp > 0):
                    load_lists(start, i, (self_src, self_dst, self_w))
                with sp.Else():
                    load_lists(start, i, (src, dst, edge_weight))

            for n in range(13):
                if n >= 2:
                    sp.wait_ge(s_wlo, n - 1)
                if n == 0:
                    sp.dma_start(nat[:, 0, 0:KT * D].rearrange("p (k d) -> p k d", k=KT),
                                 W.rearrange("(k p) d -> p k d", p=P)).then_inc(s_wraw[0], 16)
                    continue
                layer, pair = divmod(n - 1, 4)
                w = (W1, W2, Wo)[layer][2 * pair:2 * pair + 2]
                sp.dma_start(nat[:, n % 2, :].rearrange("p (e k d) -> p e k d", e=2, k=KT),
                             w.rearrange("e (k p) d -> p e k d", p=P)).then_inc(s_wraw[n % 2], 16)

            x_t = x.rearrange("(g t p) d -> g p t d", t=GT, p=NT)
            out_t = out.rearrange("(g t p) d -> g p t d", t=GT, p=NT)

            def load_x1(g):
                sp.dma_start(x1[:], x_t[bass.ds(g, 1)].rearrange("o p t d -> (o p) t d")).then_inc(s_x1in, 16)

            load_x1(0)
            for tile in range(GT, GT + 2 + AHEAD):
                sp.wait_ge(s_piece, PT * (tile - GT + 1))
                load_window(tile, tile % GT)

            def store_y(g):
                sp.wait_ge(s_y, GT * E * g + GT * E)
                sp.dma_start(out_t[bass.ds(g, 1)].rearrange("o p t d -> (o p) t d"), y).then_inc(s_out, 16)

            def body(g, parts, first=False):
                for s in range(0, E, 2):
                    if s == 2 and not first:
                        store_y(g - 1)
                    if parts == FULL:
                        tile = 2 + AHEAD + s // 2
                        sp.wait_ge(s_piece, PT * GT * g + PT * (tile + 1))
                        load_window(GT * g + GT + tile, tile % GT)
                    if parts[2] and s == 2:
                        sp.wait_ge(s_y, GT * E * g + GT)
                        load_x1(g + 1)

            body(0, FULL, first=True)
            with sp.Fori(1, G - 2) as g:
                body(g, FULL)
            body(G - 2, NO_SECOND)
            body(G - 1, LAST)
            store_y(G - 1)
            sp.wait_ge(s_out, 16 * G)

        @block.gpsimd
        def _(pool):
            nc.gpsimd.iota(node_i[:], pattern=[[1, NT]], base=0, channel_multiplier=0)
            nc.gpsimd.iota(thr_i[:], pattern=[[NT, TILES]], base=0, channel_multiplier=0)
            nc.gpsimd.iota(thrp_i[:], pattern=[[0, 1]], base=0, channel_multiplier=NT)
            nc.gpsimd.iota(part_i[:], pattern=[[0, 1]], base=0, channel_multiplier=1)
            nc.gpsimd.memset(next_i[:], N)
            nc.gpsimd.memset(start_row[:], float(NE))
            nc.gpsimd.memset(ones[:], 1.0)
            nc.gpsimd.memset(eps[:, 0:1], LN_EPS)
            nc.gpsimd.memset(eps[:, 1:2], BN_EPS)
            nc.gpsimd.memset(ident[:], 0.0).then_inc(s_zero, 1)
            pool.wait_ge(s_zero, 1)
            nc.gpsimd.affine_select(out=ident[:], in_=ident[:], compare_op=ALU.not_equal, fill=1.0, base=0,
                                    pattern=[[-1, P]], channel_multiplier=1).then_inc(s_const, 1)
            pool.wait_ge(s_row_i, 1)
            pool.indirect_dma_start(out=dstrows[0:TILES, :], out_offset=None,
                                    in_=dst.rearrange("(r c) -> r c", c=COLS),
                                    in_offset=bass.IndirectOffsetOnAxis(ap=row_i[0:TILES, :], axis=0),
                                    ).then_inc(s_dstrows, 16)
            for c in range(XC):
                pool.wait_ge(s_stat, c + 1)
                row = xbuf[0:NT, c % XB, (XN - 1) * D:XN * D]
                j = (c + 1) * XN - 1
                nc.gpsimd.tensor_scalar(row, row, affine[0:NT, 0, j:j + 1], affine[0:NT, 1, j:j + 1],
                                        ALU.mult, ALU.add).then_inc(s_norm_last, 1)
            for i in range(XB):
                pool.wait_ge(s_xout[i], 16 * len(range(i, XC, XB)))

            pool.wait_ge(s_flag, 1)
            general_pool = pool.value_load(general[0:1, 0:1], min_val=0, max_val=1)
            with pool.If(general_pool > 0):
                nc.gpsimd.iota(self_i[:, 0, :], pattern=[[1, SELF]], base=0, channel_multiplier=SELF)
                nc.gpsimd.memset(self_f[:], 1.0).then_inc(s_gself, 1)
                pool.wait_ge(s_gzeroed, 16 * 11)
                with pool.Fori(0, NE // SE) as c:
                    pool.wait_ge(s_gin, c * 64 + 64)
                    pool.sem_inc(s_go, 1)
                    pool.indirect_dma_start(out=gath[0:SE, 0, 0, :], out_offset=None, in_=xn_table,
                                            in_offset=bass.IndirectOffsetOnAxis(ap=edge_i[:, 0:1], axis=0),
                                            ).then_inc(s_grow, 16)
                    pool.wait_ge(s_gsum, c + 1)
                    pool.sem_inc(s_go, 1)
                    pool.indirect_dma_start(out=sum_table, out_offset=bass.IndirectOffsetOnAxis(
                                                ap=edge_i[:, 2:3], axis=0),
                                            in_=gath[0:SE, 1, 0, :], in_offset=None,
                                            compute_op=ALU.add).then_inc(s_gadd, 16)
                pool.wait_ge(s_gcopy, 16 * 4)

            def gather(g, r):
                tile, u = r // PT, r % PT
                if u == 0:
                    pool.wait_ge(s_win[tile], 48 * g + 48)
                whole = isinstance(g, int) and PG * g + r - GR < LEAD
                if not whole:
                    pool.wait_ge(s_rlo, split_count(g, (r - GR - LEAD) // PS, r % PS))
                elif not (isinstance(g, int) and PG * g + r < GR):
                    pool.wait_ge(s_piece, PG * g + r - GR + 1)
                pool.sem_inc(s_go, 1)
                for c in range(PC):
                    pool.indirect_dma_start(out=gath[:, r % GR, c, :], out_offset=None, in_=xn_table,
                                            in_offset=bass.IndirectOffsetOnAxis(
                                                ap=idx[:, tile, u * PC + c:u * PC + c + 1], axis=0),
                                            ).then_inc(s_gath[r % GR], 16)

            for g in range(2):
                for r in range(PG):
                    gather(g, r)
            with pool.Fori(2, G) as g:
                for r in range(PG):
                    gather(g, r)

        @block.scalar
        def _(act):
            xn_v = xn_table.rearrange("(p n) d -> p (n d)", p=NT)
            def deviations(n, half, wanted):
                act.wait_ge(s_var, wanted)
                nc.scalar.activation(small[0:NT, half, 3, 0:n], small[0:NT, half, 2, 0:n], ACT.Sqrt,
                                     bias=eps[0:NT, 0:1]).then_inc(s_dev, 1)

            deviations(XN, 0, 1)
            for c in range(XC):
                if c + 1 < XC:
                    deviations(XN, (c + 1) % 2, c + 2)
                act.wait_ge(s_stat, c + 1)
                for n in range(XN - 1):
                    j = c * XN + n
                    last = nc.scalar.activation(xbuf[0:NT, c % XB, n * D:(n + 1) * D],
                                                xbuf[0:NT, c % XB, n * D:(n + 1) * D], ACT.Identity,
                                                bias=affine[0:NT, 1, j:j + 1], scale=affine[0:NT, 0, j:j + 1])
                last.then_inc(s_norm, 1)
                act.wait_ge(s_norm, c + 1)
                act.wait_ge(s_norm_last, c + 1)
                act.dma_start(xn_v[:, c * XN * D:(c + 1) * XN * D], xbuf[0:NT, c % XB, :]).then_inc(s_xout[c % XB], 16)
            for n in range(2):
                act.wait_ge(s_bnvar, n + 1)
                vv = bn_col[n][:, (NPAR - 1) * E * KT:]
                nc.scalar.activation(vv, vv, ACT.Sqrt, bias=eps[:, 1:2]).then_inc(s_bndev, 1)
            act.wait_ge(s_bn, 1)
            for i in range(XB):
                act.wait_ge(s_xout[i], 16 * len(range(i, XC, XB)))

            def weights_hi(n):
                act.wait_ge(s_wraw[n % 2], 16 * (n // 2 + 1))
                if n == 0:
                    nc.scalar.copy(gw_hi[:].rearrange("p k d -> p (k d)"), nat[:, 0, 0:KT * D]).then_inc(s_whi, 1)
                    return
                layer, pair = divmod(n - 1, 4)
                nc.scalar.copy(w_hi[layer][:, 2 * pair:2 * pair + 2].rearrange("p e k d -> p (e k d)"),
                               nat[:, n % 2, :]).then_inc(s_whi, 1)

            def copy_agg(tile, i):
                act.wait_ge(s_piece, PT * tile + PT)
                nc.scalar.copy(agg[:, i, :], ps_agg[0:NT, i % 2 * D:(i % 2 + 1) * D]).then_inc(s_aggn, 1)

            def rows_hi_of(q, r, gathered):
                i, u = r // PT % GT, r % PT
                act.wait_ge(s_gath[r % GR], gathered)
                act.wait_ge(s_piece, q - SR + 1)
                for c in range(PC):
                    k = u * PC + c
                    last = nc.scalar.activation(rows_hi[:, r % SR, c, :], gath[:, r % GR, c, :], ACT.Copy,
                                                scale=win_w[:, i, k:k + 1])
                last.then_inc(s_rhi, 1)

            def slot_rows_hi(g, s, us=range(PS)):
                for u in us:
                    r = LEAD + PS * s + u
                    rows_hi_of(PG * g + r, r, gathered_count(g, r))

            def split_hi(g, done, hi, out_sem, k):
                act.wait_ge(done, KT * g + k + 1)
                nc.scalar.copy(hi[:, k, :], ps_mix[:, 0:GN]).then_inc(out_sem, 1)

            for i in range(GT):
                for n in range(3 * i, 3 * i + 3):
                    weights_hi(n)
                copy_agg(i, i)
            for k in range(KT):
                split_hi(0, s_ta, agg_hi, s_tahi, k)
            weights_hi(12)
            copy_agg(GT, 0)
            deviations(GT, 0, XC + 1)
            copy_agg(GT + 1, 1)
            for k in range(KT):
                split_hi(0, s_t2, x2_hi, s_x2hi, k)
            slot_rows_hi(0, 0)

            def hidden(g, s, layer, first):
                done, ps_in, hi, hi_done, lo_done, freed = (
                    (s_l1, ps_h1, h1_hi, s_h1, s_h1lo, s_l2), (s_l2, ps_h2, h2_hi, s_h2, s_h2lo, s_l3))[layer]
                for k in range(KT):
                    act.wait_ge(done, KT * (E * g + s) + k + 1)
                    if layer == 1:
                        act.wait_ge(s_h1lo, KT * (E * g + s) + k + 1)
                    elif not (first and s == 0):
                        act.wait_ge(s_h2lo, KT * (E * g + s - 1) + k + 1)
                    col = s * KT + k
                    nc.scalar.activation(h_full[:, k, :], ps_in[k][:, 0:GN], ACT.Relu,
                                         bias=bn_bias[layer][:, col:col + 1], scale=bn_scale[layer][:, col:col + 1])
                    if k == 0 and not (first and s == 0):
                        if layer == 0:
                            act.wait_ge(s_l2, KT * (E * g + s))
                        else:
                            act.wait_ge(s_l3, GT * (E * g + s))
                    nc.scalar.activation(hi[:, k, :], ps_in[k][:, 0:GN], ACT.Relu,
                                         bias=bn_bias[layer][:, col:col + 1],
                                         scale=bn_scale[layer][:, col:col + 1]).then_inc(hi_done, 1)

            def body(g, parts, first=False):
                def copy_done(s):
                    if has_pieces(parts, s) and s % 2 == 1:
                        i = (s // 2 + 2) % GT
                        if i == 0:
                            act.wait_ge(s_ta, KT * g + 2 * KT)
                        copy_agg(GT * g + GT + 2 + s // 2, i)

                for s in range(E):
                    now = [(s + 1, u) for u in range(PS) if s < E - 1 and has_pieces(parts, s + 1)]
                    if parts == FULL and s == E - 2:
                        now.pop()
                    if parts == FULL and s == E - 1:
                        now = [(E - 1, 2), (E, 0), (E, 1), (E, 2)]

                    def rows(n):
                        for of, u in now[:n]:
                            slot_rows_hi(g, of, [u])
                        del now[:n]

                    hidden(g, s, 0, first)
                    if s < E - 1:
                        copy_done(s)
                    if parts[2] and s == 6:
                        deviations(GT, 0, g + XC + 2)
                    if parts[2] and s == 7:
                        split_hi(g + 1, s_t2, x2_hi, s_x2hi, 0)
                    rows(1)
                    if parts[2] and s == 4:
                        split_hi(g + 1, s_ta, agg_hi, s_tahi, 0)
                    if s < E - 1:
                        rows(1)
                    if s == 0:
                        act.wait_ge(s_lgs, g + 1)
                        nc.scalar.activation(probs[:], probs[:], ACT.Exp).then_inc(s_exp, 1)
                    if parts[2] and s == 4:
                        split_hi(g + 1, s_ta, agg_hi, s_tahi, 1)
                    if parts[2] and s == 7:
                        split_hi(g + 1, s_t2, x2_hi, s_x2hi, 1)
                        copy_done(s)
                    rows(1)
                    if s == 1:
                        act.wait_ge(s_pt, g + 1)
                        nc.scalar.copy(probs_t[:].rearrange("e t n -> e (t n)"), ps_mix[0:3 * E, 0:GN]).then_inc(s_pts, 1)
                    hidden(g, s, 1, first)
                    rows(2)

            body(0, FULL, first=True)
            with act.Fori(1, G - 2) as g:
                body(g, FULL)
            body(G - 2, NO_SECOND)
            body(G - 1, LAST)

        @block.vector
        def _(dve):
            steps = [0]

            def setup(ins):
                ins.then_inc(s_setup, 1)
                steps[0] += 1
                dve.wait_ge(s_setup, steps[0])

            v = nc.vector
            dve.wait_ge(s_const, 1)
            setup(v.tensor_copy(node_f[:], node_i[:]))
            setup(v.tensor_copy(thr_f[:], thr_i[:]))
            dve.wait_ge(s_first, 16)
            setup(v.tensor_copy(find[0:ROWS, 0:1], first_i[0:ROWS, :]))
            v.tensor_scalar(row_hit[0:ROWS, :], thr_f[0:ROWS, :], find[0:ROWS, 0:1], None,
                            ALU.is_gt).then_inc(s_hit, 1)
            dve.wait_ge(s_rows, 1)
            setup(v.tensor_scalar(find[0:TILES, 1:2], ps_mix[0:TILES, 0:1], -1.0, 0.0, ALU.add, ALU.max))
            v.tensor_copy(row_i[0:TILES, :], find[0:TILES, 1:2]).then_inc(s_row_i, 1)
            setup(v.tensor_copy(find[0:TILES, 2:3], thrp_i[0:TILES, :]))

            def layer_norm_stats(n, half, src_of, link):
                for m in range(n):
                    last = v.bn_stats(stat[0:NT, m, :], src_of(m))
                link(last)
                st = stat[0:NT, 0:n, :]
                sm = [small[0:NT, half, q, 0:n] for q in range(4)]
                v.tensor_tensor(sm[0], st[:, :, 1], st[:, :, 4], ALU.add)
                v.tensor_tensor(sm[1], st[:, :, 1], st[:, :, 4], ALU.subtract)
                link(v.tensor_tensor(sm[2], st[:, :, 2], st[:, :, 5], ALU.add))
                link(v.scalar_tensor_tensor(sm[3], sm[1], 0.25, sm[1], ALU.mult, ALU.mult))
                return v.scalar_tensor_tensor(sm[2], sm[2], 1.0 / D, sm[3], ALU.mult, ALU.add)

            def layer_norm_affine(n, half, j, link):
                sm = [small[0:NT, half, q, 0:n] for q in range(4)]
                link(v.reciprocal(affine[0:NT, 0, j:j + n], sm[3]))
                return v.scalar_tensor_tensor(affine[0:NT, 1, j:j + n], sm[0], -0.5, affine[0:NT, 0, j:j + n],
                                              ALU.mult, ALU.mult)

            for c in range(XC + 1):
                if c < XC:
                    dve.wait_ge(s_xin[c % XB], 16 * (c // XB + 1))
                    layer_norm_stats(XN, c % 2, lambda m: xbuf[0:NT, c % XB, m * D:(m + 1) * D],
                                     setup).then_inc(s_var, 1)
                if c > 0:
                    dve.wait_ge(s_dev, c)
                    layer_norm_affine(XN, (c - 1) % 2, (c - 1) * XN, setup).then_inc(s_stat, 1)
                if c == 3:
                    dve.wait_ge(s_dstrows, 16)
                    setup(v.tensor_scalar(below[0:TILES, :], dstrows[0:TILES, :], find[0:TILES, 2:3], None, ALU.is_lt))
                if c == 4:
                    setup(v.tensor_reduce(find[0:TILES, 3:4], below[0:TILES, :], AX_X, ALU.add))
                if c == 5:
                    dve.wait_ge(s_whole, 32)
                    setup(v.tensor_tensor(below[0:ROWS, 0:COLS - 1], dst_all[:, 1:COLS], dst_all[:, 0:COLS - 1],
                                          ALU.is_lt))
                if c == 6:
                    v.tensor_reduce(find[0:ROWS, 6:7], below[0:ROWS, 0:COLS - 1], AX_X, ALU.max)
                    setup(v.tensor_tensor(find[0:ROWS, 7:8], next_i[:], dst_all[:, COLS - 1:COLS], ALU.is_lt))
                    setup(v.tensor_tensor(find[0:ROWS, 8:9], find[0:ROWS, 6:7], find[0:ROWS, 7:8], ALU.add))
                if c == 7:
                    setup(v.scalar_tensor_tensor(find[0:TILES, 4:5], find[0:TILES, 1:2], float(COLS),
                                                 find[0:TILES, 3:4], ALU.mult, ALU.add))
                    v.tensor_scalar(find[0:TILES, 5:6], find[0:TILES, 4:5], float(NE - WIN), None,
                                    ALU.min).then_inc(s_start, 1)
                if c == 8:
                    dve.wait_ge(s_start_t, 1)
                    setup(v.tensor_copy(find[0:1, 9:10], ps_mix[0:1, 2 * P:2 * P + 1]))
                    setup(v.tensor_copy(start_row[:, 0, 0:TILES], ps_mix[0:1, P:P + TILES]))
                    v.tensor_copy(starts[:], ps_mix[0:1, 0:TILES]).then_inc(s_starts, 1)
                if c == 9:
                    setup(v.tensor_tensor(start_row[:, 1, 0:TILES], start_row[:, 0, 1:TILES + 1],
                                          start_row[:, 0, 0:TILES], ALU.subtract))
                    setup(v.tensor_reduce(find[0:1, 10:11], start_row[:, 1, 0:TILES], AX_X, ALU.max))
                    setup(v.tensor_scalar(find[0:1, 10:11], find[0:1, 10:11], float(WIN), None, ALU.is_gt))
                    setup(v.tensor_scalar(find[0:1, 9:10], find[0:1, 9:10], 0.0, None, ALU.is_gt))
                    v.tensor_tensor(general[:], find[0:1, 9:10], find[0:1, 10:11], ALU.max).then_inc(s_flag, 1)
            dve.wait_ge(s_bnt, 1)
            for n in range(2):
                v.tensor_copy(bn_col[n][:], ps_mix[:, n * D:n * D + NPAR * E * KT]).then_inc(s_bnvar, 1)
                bb, gg, be, mm, vv = (bn_col[n][:, q * E * KT:(q + 1) * E * KT] for q in range(NPAR))
                dve.wait_ge(s_bndev, n + 1)
                setup(v.reciprocal(vv, vv))
                setup(v.tensor_tensor(bn_scale[n][:], gg, vv, ALU.mult))
                setup(v.tensor_tensor(bb, bb, mm, ALU.subtract))
                setup(v.tensor_tensor(bb, bb, bn_scale[n][:], ALU.mult))
                last = v.tensor_tensor(bn_bias[n][:], bb, be, ALU.add)
            last.then_inc(s_bn, 1)
            v.tensor_copy(ones_r[:], ones[0:2, 0:NT])
            v.tensor_copy(b_half[:, 0, :], b_row[:])
            v.tensor_copy(bo_half[:, 0, :], bo_sb[:])
            setup(v.tensor_copy(wr_pair[:, :, 0, :], wr_sb[:]))
            v.tensor_tensor(b_half[:, 1, :], b_row[:], b_half[:, 0, :].bitcast(F32), ALU.subtract)
            v.tensor_tensor(bo_half[:, 1, :], bo_sb[:], bo_half[:, 0, :].bitcast(F32), ALU.subtract)
            setup(v.tensor_tensor(wr_pair[:, :, 1, :], wr_sb[:], wr_pair[:, :, 0, :].bitcast(F32), ALU.subtract))
            v.tensor_copy(find[0:1, 6:7], find[0:1, 5:6]).then_inc(s_halves, 1)
            dve.wait_ge(s_flag, 1)
            general_dve = dve.value_load(general[0:1, 0:1], min_val=0, max_val=1)
            with dve.If(general_dve > 0):
                v.memset(gath[:], 0.0).then_inc(s_gzero, 1)
                dve.wait_ge(s_gself, 1)
                v.tensor_scalar(self_i[:, 1, :], self_i[:, 0, :], float(N - 1), None, ALU.min).then_inc(s_gself, 1)
                dve.wait_ge(s_starts, 1)
                v.tensor_copy(starts[:], thr_i[0:1, :]).then_inc(s_gstarts, 1)
                v.tensor_copy(edge_f[:, 0:1], part_i[0:SE, :]).then_inc(s_gstep, 1)
                dve.wait_ge(s_gstep, 1)
                v.tensor_scalar(same[:, 0, :], node_f[0:SE, 0:SE], edge_f[:, 0:1], None, ALU.is_lt)
                v.tensor_scalar(edge_f[:, 1:2], edge_f[:, 0:1], float(N), None, ALU.add).then_inc(s_gstep, 1)
                dve.wait_ge(s_gstep, 2)
                with dve.Fori(0, NE // SE) as c:
                    done = [0]

                    def glink(ins):
                        ins.then_inc(s_gloop, 1)
                        done[0] += 1
                        dve.wait_ge(s_gloop, c * 6 + done[0])

                    dve.wait_ge(s_gin, c * 64 + 64)
                    glink(v.tensor_copy(edge_f[:, 2:3], edge_i[:, 1:2]))
                    glink(v.tensor_scalar(same[:, 1, :], dst_row[:], edge_f[:, 2:3], None, ALU.is_equal))
                    v.tensor_scalar(same[:, 2, :], dst_row[:], edge_f[:, 2:3], edge_w[:], ALU.is_equal, ALU.mult)
                    glink(v.tensor_tensor(same[:, 3, :], same[:, 1, :], same[:, 0, :], ALU.mult))
                    glink(v.tensor_reduce(edge_f[:, 3:4], same[:, 3, :], AX_X, ALU.max))
                    glink(v.tensor_tensor(edge_f[:, 4:5], edge_f[:, 1:2], edge_f[:, 2:3], ALU.subtract))
                    glink(v.tensor_tensor(edge_f[:, 5:6], edge_f[:, 4:5], edge_f[:, 3:4], ALU.mult))
                    v.tensor_tensor(edge_i[:, 2:3], edge_f[:, 5:6], edge_f[:, 2:3], ALU.add).then_inc(s_gsame, 1)
                    dve.wait_ge(s_gmm, c + 1)
                    v.tensor_copy(gath[0:SE, 1, 0, :], ps_mix[0:SE, 0:D]).then_inc(s_gsum, 1)
                    assert done[0] == 6

            def stage(g, tile, i):
                dve.wait_ge(s_win[i], 48 * g + 48)
                return v.tensor_scalar(rel[:, i, :], win_dst[:, i, :], thr_f[:, bass.ds(tile, 1)], None, ALU.subtract)

            def onehot_weighted(q, r):
                i, u = r // PT % GT, r % PT
                dve.wait_ge(s_piece, q - SR + 1) if not (isinstance(q, int) and q < SR) else None
                for c in range(PC):
                    k = u * PC + c
                    last = v.tensor_scalar(hot[:, r % SR, c, :], node_f[:], rel[:, i, k:k + 1],
                                           win_w[:, i, k:k + 1], ALU.is_equal, ALU.mult)
                last.then_inc(s_hot, 1)

            def onehot_of_split(q, r):
                i, u = r // PT % GT, r % PT
                dve.wait_ge(s_piece, q - SR + 1)
                v.tensor_tensor(hot_r[:, r % SR, :, :], node_f[:].unsqueeze(1).broadcast_to([P, PC, NT]),
                                rel[:, i, u * PC:(u + 1) * PC].unsqueeze(2).broadcast_to([P, PC, NT]),
                                ALU.is_equal).then_inc(s_hot, 1)

            def rows_lo_of(r, c, split):
                i, k = r // PT % GT, r % PT * PC + c
                if c == 0:
                    dve.wait_ge(s_rhi, split)
                last = v.scalar_tensor_tensor(rows_lo[:, r % SR, c, :], gath[:, r % GR, c, :],
                                              win_w[:, i, k:k + 1], rows_hi[:, r % SR, c, :].bitcast(F32),
                                              ALU.mult, ALU.subtract)
                if c == PC - 1:
                    last.then_inc(s_rlo, 1)

            def slot_steps(g, s):
                steps = [(onehot_of_split, (PG * g + LEAD + PS * s + u, LEAD + PS * s + u)) for u in range(PS)]
                return steps + [(rows_lo_of, (LEAD + PS * s + u, c, split_count(g, s, u)))
                                for u in range(PS) for c in range(PC)]

            def run(steps, count):
                for step, args in steps[:count]:
                    step(*args)
                del steps[:count]

            def lo_half(lo, whole, hi, lo_done):
                v.tensor_tensor(lo, whole, hi.bitcast(F32), ALU.subtract).then_inc(lo_done, 1)

            def add_x1(g, i):
                dve.wait_ge(s_wp, 2 * g + i + 1)
                v.tensor_tensor(x1[:, 2 * i:2 * i + 2, :], ps_mix[0:NT, :].rearrange("p (t d) -> p t d", t=2),
                                x1[:, 2 * i:2 * i + 2, :], ALU.add).then_inc(s_x1, 1)

            def norm(g):
                if not (isinstance(g, int) and g == 0):
                    dve.wait_ge(s_t2, KT * g)
                for i in range(GT):
                    last = v.tensor_scalar(xn2[:, i, :], x1[:, i, :], affine[0:NT, 0, i:i + 1],
                                           affine[0:NT, 1, i:i + 1], ALU.mult, ALU.add)
                last.then_inc(s_xn2, 1)

            weights_left = list(range(13))

            def split_weights():
                n = weights_left.pop(0)
                dve.wait_ge(s_whi, n + 1)
                if n == 0:
                    lo_half(gw_lo[:].rearrange("p k d -> p (k d)"), nat[:, 0, 0:KT * D],
                            gw_hi[:].rearrange("p k d -> p (k d)"), s_wlo)
                    return
                layer, pair = divmod(n - 1, 4)
                lo_half(w_lo[layer][:, 2 * pair:2 * pair + 2].rearrange("p e k d -> p (e k d)"), nat[:, n % 2, :],
                        w_hi[layer][:, 2 * pair:2 * pair + 2].rearrange("p e k d -> p (e k d)"), s_wlo)

            def pieces(tiles):
                for tile in tiles:
                    setup(stage(tile // GT, tile, tile % GT))
                    for u in range(PT):
                        onehot_weighted(tile * PT + u, tile * PT + u)
                        if weights_left and u < 3:
                            split_weights()

            pieces(range(GT))
            for k in range(KT):
                dve.wait_ge(s_tahi, k + 1)
                lo_half(agg_lo[:, k, :], ps_mix[:, 0:GN], agg_hi[:, k, :], s_talo)
            pieces(range(GT, GT + 1))
            dve.wait_ge(s_x1in, 16)
            for i in range(2):
                add_x1(0, i)
            dve.wait_ge(s_x1, 2)
            layer_norm_stats(GT, 0, lambda m: x1[:, m, :], setup).then_inc(s_var, 1)
            dve.wait_ge(s_dev, XC + 1)
            setup(layer_norm_affine(GT, 0, 0, setup))
            norm(0)
            pieces(range(GT + 1, GT + 2))
            setup(stage(1, GT + 2, 2))
            for k in range(KT):
                dve.wait_ge(s_x2hi, k + 1)
                lo_half(x2_lo[:, k, :], ps_mix[:, 0:GN], x2_hi[:, k, :], s_x2lo)
            run(slot_steps(0, 0), PS + PS * PC)

            def add_y(g, e, half, first=False):
                if e == 0 and half == 0 and not first:
                    dve.wait_ge(s_out, 16 * g)
                dve.wait_ge(s_l3, GT * (E * g + e) + 2 * half + 2)
                for i in range(2 * half, 2 * half + 2):
                    into = x1[:, i, :] if e == 0 else y[:, i, :]
                    v.scalar_tensor_tensor(y[:, i, :], ps_y[half][0:NT, i % 2 * D:(i % 2 + 1) * D],
                                           probs[:, i, e:e + 1], into, ALU.mult, ALU.add).then_inc(s_y, 1)

            def body(g, parts, base, first=False):
                done = [0]

                def link(ins):
                    ins.then_inc(s_step, 1)
                    done[0] += 1
                    dve.wait_ge(s_step, base + done[0])

                def link_after(ins, other_steps, count):
                    ins.then_inc(s_step, 1)
                    done[0] += 1
                    run(other_steps, count)
                    dve.wait_ge(s_step, base + done[0])

                def hidden_lo(s, layer, k):
                    hi, lo, hi_done, lo_done = ((h1_hi, h1_lo, s_h1, s_h1lo), (h2_hi, h2_lo, s_h2, s_h2lo))[layer]
                    dve.wait_ge(hi_done, KT * (E * g + s) + k + 1)
                    lo_half(lo[:, k, :], h_full[:, k, :], hi[:, k, :], lo_done)

                def softmax_shift():
                    dve.wait_ge(s_lg, g + 1)
                    if not first:
                        dve.wait_ge(s_y, GT * E * g)
                    halves = ps_mix[0:NT, 0:GT * 2 * E].rearrange("p (t h e) -> p t h e", h=2, e=E)
                    bias = br_all[:].unsqueeze(1).broadcast_to([NT, GT, E])
                    link(v.tensor_tensor(probs[:], halves[:, :, 0, :], bias, ALU.add))
                    link(v.tensor_tensor(probs[:], halves[:, :, 1, :], probs[:], ALU.add))
                    link(v.tensor_reduce(psmall[:, 0, :], probs[:], AX_X, ALU.max))
                    v.tensor_tensor(probs[:], probs[:], psmall[:, 0, :].unsqueeze(2).broadcast_to([NT, GT, E]),
                                    ALU.subtract).then_inc(s_lgs, 1)

                def softmax_sums(steps):
                    dve.wait_ge(s_exp, g + 1)
                    link_after(v.tensor_reduce(psmall[:, 1, :], probs[:], AX_X, ALU.add), steps, 1)
                    link_after(v.reciprocal(psmall[:, 1, :], psmall[:, 1, :]), steps, 1)

                def softmax_scale():
                    link(v.tensor_tensor(probs[:], probs[:], psmall[:, 1, :].unsqueeze(2).broadcast_to([NT, GT, E]),
                                         ALU.mult))
                    link(v.tensor_copy(probs_hi[:], probs[:]))
                    v.tensor_copy(probs_three[:, :, 0, :], probs_hi[:].bitcast(F32))
                    v.tensor_copy(probs_three[:, :, 2, :], probs_hi[:].bitcast(F32))
                    v.tensor_tensor(probs_three[:, :, 1, :], probs[:], probs_hi[:].bitcast(F32),
                                    ALU.subtract).then_inc(s_prob, 1)

                def add_bo(i):
                    dve.wait_ge(s_bo, 2 * g + i + 1)
                    dve.wait_ge(s_y, GT * E * g + (i + 1) * GT)
                    v.tensor_tensor(y[:, 2 * i:2 * i + 2, :], ps_mix[0:NT, :].rearrange("p (t d) -> p t d", t=2),
                                    y[:, 2 * i:2 * i + 2, :], ALU.add).then_inc(s_boy, 1)

                def sum_steps(s):
                    if not (parts == FULL if s == E else has_pieces(parts, s)):
                        return []
                    if s % 2 == 0:
                        tile = 2 + s // 2
                        link(stage(g + 1 + tile // GT, GT * g + GT + tile, tile % GT))
                    return slot_steps(g, s)

                def lo_of_agg(k):
                    dve.wait_ge(s_tahi, KT * g + KT + k + 1)
                    lo_half(agg_lo[:, k, :], ps_mix[:, 0:GN], agg_hi[:, k, :], s_talo)

                def lo_of_x2(k):
                    dve.wait_ge(s_x2hi, KT * g + KT + k + 1)
                    lo_half(x2_lo[:, k, :], ps_mix[:, 0:GN], x2_hi[:, k, :], s_x2lo)

                steps = []
                for s in range(E):
                    steps += sum_steps(s + 1) if s < E - 1 else []
                    hidden_lo(s, 0, 0)
                    if 0 < s < E - 1:
                        run(steps, 1)
                    hidden_lo(s, 0, 1)
                    if s == 0:
                        if not first:
                            for half in range(2):
                                add_y(g - 1, E - 1, half)
                        run(steps, PS)
                        softmax_shift()
                    if parts[2] and s == 6:
                        dve.wait_ge(s_dev, g + XC + 2)
                        link_after(layer_norm_affine(GT, 0, 0, lambda ins: link_after(ins, steps, 1)), steps, 1)
                        norm(g + 1)
                    if parts[2] and s == 7:
                        lo_of_x2(0)
                    if s == 2:
                        add_bo(0)
                        dve.wait_ge(s_boy, 2 * g + 1)
                    if 0 < s < E - 1:
                        run(steps, max(len(steps) - PS * PC, 0))
                    if parts[2] and s == 4:
                        lo_of_agg(0)
                    run(steps, 0 if s == E - 2 else 2 * PC if s == E - 1 else PC)
                    if s == 3:
                        add_bo(1)
                        dve.wait_ge(s_boy, 2 * g + 2)
                    if parts[2] and s == 5:
                        dve.wait_ge(s_x1in, 16 * g + 32)
                        add_x1(g + 1, 0)
                    if s > 0:
                        add_y(g, s - 1, 0, first)
                    if s < E - 2:
                        run(steps, PC)
                    if s == E - 2:
                        hidden_lo(s, 1, 0)
                    if s > 0:
                        add_y(g, s - 1, 1)
                    if parts[2] and s == 4:
                        lo_of_agg(1)
                    if parts[2] and s == 5:
                        add_x1(g + 1, 1)
                    if parts[2] and s == 7:
                        lo_of_x2(1)
                    if s == E - 1:
                        steps = sum_steps(E)
                        run(steps, PS)
                    if s == 0:
                        softmax_sums(steps)
                    if s == 1:
                        run(steps, 1)
                    if s != E - 2:
                        hidden_lo(s, 1, 0)
                        run(steps, PC if s == 2 else 2)
                    hidden_lo(s, 1, 1)
                    run(steps, PC if s == E - 2 else PS * PC)
                    if s == 0:
                        softmax_scale()
                    if parts[2] and s == 5:
                        dve.wait_ge(s_x1, 2 * g + 4)
                        layer_norm_stats(GT, 0, lambda m: x1[:, m, :], link).then_inc(s_var, 1)
                if parts == FULL:
                    assert done[0] == BODY_STEPS, done
                return done[0]

            body(0, FULL, 0, first=True)
            with dve.Fori(1, G - 2) as g:
                body(g, FULL, g * BODY_STEPS)
            n = body(G - 2, NO_SECOND, (G - 2) * BODY_STEPS)
            body(G - 1, LAST, (G - 2) * BODY_STEPS + n)
            for half in range(2):
                add_y(G - 1, E - 1, half)

        @block.tensor
        def _(pe):
            mm = nc.tensor.matmul

            pe.wait_ge(s_hit, 1)
            mm(ps_mix[0:TILES, 0:1], row_hit[0:ROWS, :], ones[0:ROWS, 0:1], start=True, stop=True).then_inc(s_rows, 1)
            pe.wait_ge(s_start, 1)
            mm(ps_mix[0:1, 0:TILES], find[0:TILES, 5:6], ident[0:TILES, 0:TILES], start=True, stop=True)
            mm(ps_mix[0:1, P:P + TILES], find[0:TILES, 4:5], ident[0:TILES, 0:TILES], start=True, stop=True)
            mm(ps_mix[0:1, 2 * P:2 * P + 1], find[0:ROWS, 8:9], ones[0:ROWS, 0:1],
               start=True, stop=True).then_inc(s_start_t, 1)
            n_small = 2 * NPAR + 4
            pe.wait_ge(s_small, 16 * n_small)
            pe.wait_ge(s_starts, 1)
            rows = NPAR * E * KT
            for n in range(2):
                last = mm(ps_mix[:, n * D:n * D + rows], bn_row[n][:], ident[0:rows, 0:rows], start=True, stop=True)
            last.then_inc(s_bnt, 1)
            pe.wait_ge(s_bn, 1)

            pe.wait_ge(s_flag, 1)
            general_pe = pe.value_load(general[0:1, 0:1], min_val=0, max_val=1)
            with pe.If(general_pe > 0):
                with pe.Fori(0, NE // SE) as c:
                    pe.wait_ge(s_grow, c * 16 + 16)
                    pe.wait_ge(s_gsame, c + 1)
                    mm(ps_mix[0:SE, 0:D], same[:, 2, :], gath[0:SE, 0, 0, :], start=True, stop=True).then_inc(s_gmm, 1)

            def product(out, hi_l, lo_l, hi_r, lo_r, start=True, stop=True):
                mm(out, hi_l, hi_r, start=start, stop=False)
                mm(out, hi_l, lo_r, start=False, stop=False)
                return mm(out, lo_l, hi_r, start=False, stop=stop)

            def sum_piece(q, r, gathered, split=None):
                tile, u = r // PT, r % PT
                o = ps_agg[0:NT, tile % 2 * D:(tile % 2 + 1) * D]
                pe.wait_ge(s_hot, q + 1)
                if split is None:
                    pe.wait_ge(s_gath[r % GR], gathered)
                    for c in range(PC):
                        last = mm(o, hot[:, r % SR, c, :], gath[:, r % GR, c, :],
                                  start=(u == 0 and c == 0), stop=(u == PT - 1 and c == PC - 1))
                else:
                    pe.wait_ge(s_rhi, split)
                    for c in range(PC):
                        mm(o, hot_r[:, r % SR, c, :], rows_hi[:, r % SR, c, :],
                           start=(u == 0 and c == 0), stop=False)
                    pe.wait_ge(s_rlo, split)
                    for c in range(PC):
                        last = mm(o, hot_r[:, r % SR, c, :], rows_lo[:, r % SR, c, :],
                                  start=False, stop=(u == PT - 1 and c == PC - 1))
                last.then_inc(s_piece, 1)

            def transpose_block(src_of, k, done):
                for i in range(GT):
                    last = nc.tensor.transpose(ps_mix[:, i * NT:(i + 1) * NT], src_of[:, i, k * P:(k + 1) * P],
                                               ident[0:NT, 0:NT])
                last.then_inc(done, 1)

            def w_product(i):
                for t in range(2):
                    tile = slice((2 * i + t) * NT, (2 * i + t + 1) * NT)
                    o = ps_mix[0:NT, t * D:(t + 1) * D]
                    mm(o, ones_r[:], b_pair[:], start=True, stop=False)
                    for k in range(KT):
                        last = product(o, agg_hi[:, k, tile], agg_lo[:, k, tile], gw_hi[:, k, :], gw_lo[:, k, :],
                                       start=False, stop=k == KT - 1)
                last.then_inc(s_wp, 1)

            for r in range(PG):
                if r >= PT and r % PT == 0:
                    pe.wait_ge(s_aggn, r // PT)
                sum_piece(r, r, gathered_count(0, r))
            pe.wait_ge(s_aggn, GT)
            transpose_block(agg, 0, s_ta)
            pe.wait_ge(s_talo, 1)
            transpose_block(agg, 1, s_ta)
            for r in range(PG, PG + PT):
                sum_piece(r, r, gathered_count(0, r))
            pe.wait_ge(s_talo, 2)
            pe.wait_ge(s_wlo, 1)
            pe.wait_ge(s_stacked, 16 * 5)
            w_product(0)
            pe.wait_ge(s_x1, 1)
            w_product(1)
            pe.wait_ge(s_aggn, GT + 1)
            for r in range(PG + PT, LEAD):
                sum_piece(r, r, gathered_count(0, r))
            pe.wait_ge(s_xn2, 1)
            transpose_block(xn2, 0, s_t2)
            pe.wait_ge(s_x2lo, 1)
            transpose_block(xn2, 1, s_t2)
            pe.wait_ge(s_wlo, 13)

            def output(g, e, first=False):
                for i in range(GT):
                    if i % 2 == 0 and not (first and e == 0):
                        pe.wait_ge(s_y, GT * (E * g + e) + i - 2)
                    o = ps_y[i // 2][0:NT, i % 2 * D:(i % 2 + 1) * D]
                    tile = slice(i * NT, (i + 1) * NT)
                    for k in range(KT):
                        if i == 0:
                            pe.wait_ge(s_h2, KT * (E * g + e) + k + 1)
                        mm(o, h2_hi[:, k, tile], w_hi[2][:, e, k, :], start=k == 0, stop=False)
                        mm(o, h2_hi[:, k, tile], w_lo[2][:, e, k, :], start=False, stop=False)
                        if i == 0:
                            pe.wait_ge(s_h2lo, KT * (E * g + e) + k + 1)
                        last = mm(o, h2_lo[:, k, tile], w_hi[2][:, e, k, :], start=False, stop=k == KT - 1)
                    last.then_inc(s_l3, 1)

            def body(g, parts, first=False):
                def layer(s, n):
                    ps_o, hi, lo, done = ((ps_h1, x2_hi, x2_lo, s_l1), (ps_h2, h1_hi, h1_lo, s_l2))[n]
                    if n == 0 and s == 0:
                        pe.wait_ge(s_x2lo, KT * g + KT)
                    if n == 1:
                        pe.wait_ge(s_h1lo, KT * (E * g + s) + KT)
                    if n == 0 and not (first and s == 0):
                        pe.wait_ge(s_h1, KT * (E * g + s))
                    if n == 1 and not (first and s == 0):
                        pe.wait_ge(s_h2, KT * (E * g + s))
                    for m in range(KT):
                        for k in range(KT):
                            cols = slice(m * P, (m + 1) * P)
                            last = product(ps_o[m][:, 0:GN], w_hi[n][:, s, k, cols], w_lo[n][:, s, k, cols],
                                           hi[:, k, :], lo[:, k, :], start=k == 0, stop=k == KT - 1)
                        last.then_inc(done, 1)

                def sums(s):
                    if has_pieces(parts, s):
                        if s % 2 == 0:
                            pe.wait_ge(s_aggn, GT * g + GT + s // 2 + 2)
                        for u in range(PS):
                            r = LEAD + PS * s + u
                            sum_piece(PG * g + r, r, gathered_count(g, r), split_count(g, s, u))

                def logits():
                    for i in range(GT):
                        o = ps_mix[0:NT, i * 2 * E:(i + 1) * 2 * E]
                        tile = slice(i * NT, (i + 1) * NT)
                        for k in range(KT):
                            pair = wr_pair[:, k, :, :].rearrange("p h e -> p (h e)")
                            mm(o, x2_hi[:, k, tile], pair, start=k == 0, stop=False)
                            last = mm(o, x2_lo[:, k, tile], pair, start=False, stop=k == KT - 1)
                    last.then_inc(s_lg, 1)

                def bo_product(i):
                    for t in range(2):
                        last = mm(ps_mix[0:NT, t * D:(t + 1) * D], probs_t[:, 2 * i + t, :], bo_three[:],
                                  start=True, stop=True)
                    last.then_inc(s_bo, 1)

                for s in range(E):
                    layer(s, 0)
                    if s == 0 and not first:
                        output(g - 1, E - 1)
                    if s < E - 1:
                        sums(s)
                    if s == 0:
                        logits()
                    if s == 2:
                        pe.wait_ge(s_pts, g + 1)
                        bo_product(0)
                    if parts[2] and s == 4:
                        pe.wait_ge(s_aggn, GT * g + 2 * GT)
                        pe.wait_ge(s_boy, 2 * g + 2)
                        transpose_block(agg, 0, s_ta)
                    if parts[2] and s == 5:
                        pe.wait_ge(s_talo, KT * g + 2 * KT)
                        w_product(0)
                    if parts[2] and s == 7:
                        pe.wait_ge(s_xn2, g + 2)
                        transpose_block(xn2, 0, s_t2)
                    if s > 0:
                        output(g, s - 1, first)
                    if s == 1:
                        pe.wait_ge(s_prob, g + 1)
                        for i in range(GT):
                            last = nc.tensor.transpose(ps_mix[0:3 * E, i * NT:(i + 1) * NT],
                                                       probs_three[:, i, :, :].rearrange("p h e -> p (h e)"),
                                                       ident[0:NT, 0:NT])
                        last.then_inc(s_pt, 1)
                    if s == 2:
                        pe.wait_ge(s_boy, 2 * g + 1)
                        bo_product(1)
                    if parts[2] and s == 4:
                        pe.wait_ge(s_talo, KT * g + KT + 1)
                        transpose_block(agg, 1, s_ta)
                    if parts[2] and s == 5:
                        pe.wait_ge(s_x1, 2 * g + 3)
                        w_product(1)
                    if parts[2] and s == 7:
                        pe.wait_ge(s_x2lo, KT * g + KT + 1)
                        transpose_block(xn2, 1, s_t2)
                    if s == E - 1:
                        sums(s)
                    layer(s, 1)

            body(0, FULL, first=True)
            with pe.Fori(1, G - 2) as g:
                body(g, FULL)
            body(G - 2, NO_SECOND)
            body(G - 1, LAST)
            output(G - 1, E - 1)


_INS = ["x", "src", "dst", "edge_weight", "L0_gnn_W", "L0_gnn_b", "L0_ffn_Wr", "L0_ffn_br", "L0_ffn_W1", "L0_ffn_b1",
        "L0_ffn_g1", "L0_ffn_be1", "L0_ffn_m1", "L0_ffn_v1", "L0_ffn_W2", "L0_ffn_b2", "L0_ffn_g2", "L0_ffn_be2",
        "L0_ffn_m2", "L0_ffn_v2", "L0_ffn_Wo", "L0_ffn_bo"]


def kernel(**inputs):
    import numpy as _np
    import concourse.bacc as _bacc
    from concourse import mybir as _mybir
    from concourse.bass_utils import run_bass_kernel_spmd as _run

    nc = _bacc.Bacc("TRN2", target_bir_lowering=False, num_devices=1)
    arrays, args = {}, []
    for name in _INS:
        a = _np.ascontiguousarray(inputs[name])
        arrays[f"in_{name}"] = a
        args.append(nc.dram_tensor(f"in_{name}", a.shape, _mybir.dt.from_np(a.dtype), kind="ExternalInput").ap())
    args.append(nc.dram_tensor("out_x", (N, D), F32, kind="ExternalOutput").ap())
    gnn_experts(nc, *args)
    r = _run(nc, [arrays], core_ids=[0])
    return r.results[0]["out_x"]
```
